# Optimizing a Trainium2 kernel written in Bass

```python
import numpy as np
import jax
import jax.numpy as jnp

def _softmax(x, axis=-1):
    return jax.nn.softmax(x, axis=axis)

def _gelu(x):
    return jax.nn.gelu(x, approximate=True)

def _silu(x):
    return jax.nn.silu(x)

def _sigmoid(x):
    return jax.nn.sigmoid(x)

def _layernorm(x, axis=-1, eps=1e-05):
    m = jnp.mean(x, axis=axis, keepdims=True)
    v = jnp.var(x, axis=axis, keepdims=True)
    return (x - m) / jnp.sqrt(v + eps)

def _scatter_add(tgt, idx, src, axis=0):
    return tgt.at[idx].add(src)

def _segment_sum(src, seg, n):
    return jax.ops.segment_sum(src, seg, n)
kernel_name = 'mk_adaln_d1_jaxref_r8_50c447'

def setup_inputs(seed: int=0):
    np.random.seed(seed)
    _w = jnp.asarray

    def _L0_attn_setup():
        import math
        import jax, jax.numpy as jnp
        import numpy as np
        N_HEAD = 16

        def _reference_tuple_inner(x, W_dq, W_uq, W_dkv, W_uk, W_uv, W_o):
            B, T, C = x.shape
            nh = N_HEAD
            hs = C // nh
            kvl = W_dkv.shape[0]
            k_eff = (W_dq.T @ W_uq.T @ W_uk).reshape(nh, hs, kvl)
            v_eff = (W_uv.T @ W_o.T).reshape(kvl, nh, hs).transpose(1, 0, 2)
            c_kv = x @ W_dkv.T
            q = (x @ W_dq.T @ W_uq.T).reshape(B, T, nh, hs).transpose(0, 2, 1, 3)
            q_lat = jnp.einsum('bhtd,hdl->bhtl', q, k_eff)
            attn = jnp.einsum('bhtl,bsl->bhts', q_lat, c_kv) / math.sqrt(hs)
            causal_mask = jnp.triu(jnp.ones((T, T), bool), k=1)
            attn = jnp.where(causal_mask[None, None], -jnp.inf, attn)
            attn = jax.nn.softmax(attn, axis=-1)
            ctx = jnp.einsum('bhts,bsl->bhtl', attn, c_kv)
            y = jnp.einsum('bhtl,hld->bhtd', ctx, v_eff).transpose(0, 2, 1, 3).reshape(B, T, C)
            return (y, c_kv)
        key = jax.random.key(seed)
        ks = jax.random.split(key, 7)
        B, T, C = (4, 256, 128)
        QL, KVL = (32, 32)
        s = 0.02
        return {'x': jax.random.normal(ks[0], (B, T, C), jnp.float32), 'W_dq': jax.random.normal(ks[1], (QL, C), jnp.float32) * s, 'W_uq': jax.random.normal(ks[2], (C, QL), jnp.float32) * s, 'W_dkv': jax.random.normal(ks[3], (KVL, C), jnp.float32) * s, 'W_uk': jax.random.normal(ks[4], (C, KVL), jnp.float32) * s, 'W_uv': jax.random.normal(ks[5], (C, KVL), jnp.float32) * s, 'W_o': jax.random.normal(ks[6], (C, C), jnp.float32) * s}
    _L0_attn_in = _L0_attn_setup()

    def _L0_ffn_setup():
        import jax, jax.numpy as jnp
        import numpy as np
        NUM_EXPERTS = 8
        TOP_K = 2

        def _swiglu(x, w1, w2, w3):
            return jax.nn.silu(x @ w1) * (x @ w3) @ w2
        key = jax.random.key(seed)
        ks = jax.random.split(key, 9)
        B, S, D, H, E = (1, 128, 128, 128, NUM_EXPERTS)
        std = 0.02
        return {'x': jax.random.normal(ks[0], (B, S, D), jnp.float32), 'router_w': jax.random.normal(ks[1], (D, E), jnp.float32) * std, 'expert_bias': jnp.zeros((E,), jnp.float32), 'w1': jax.random.normal(ks[2], (E, D, H), jnp.float32) * std, 'w2': jax.random.normal(ks[3], (E, H, D), jnp.float32) * std, 'w3': jax.random.normal(ks[4], (E, D, H), jnp.float32) * std, 'sw1': jax.random.normal(ks[5], (D, H), jnp.float32) * std, 'sw2': jax.random.normal(ks[6], (H, D), jnp.float32) * std, 'sw3': jax.random.normal(ks[7], (D, H), jnp.float32) * std}
    _L0_ffn_in = _L0_ffn_setup()
    _L0_c = _w((lambda *s: np.random.randn(*s).astype(np.float32) * 0.05)(8, 128))
    _L0_wmod = _w((lambda *s: np.random.randn(*s).astype(np.float32) * 0.05)(128, 6 * 128) * 128 ** (-0.5))
    _d = {'L0_attn_x': _L0_attn_in['x'], 'L0_attn_W_dq': _L0_attn_in['W_dq'], 'L0_attn_W_uq': _L0_attn_in['W_uq'], 'L0_attn_W_dkv': _L0_attn_in['W_dkv'], 'L0_attn_W_uk': _L0_attn_in['W_uk'], 'L0_attn_W_uv': _L0_attn_in['W_uv'], 'L0_attn_W_o': _L0_attn_in['W_o'], 'L0_ffn_router_w': _L0_ffn_in['router_w'], 'L0_ffn_expert_bias': _L0_ffn_in['expert_bias'], 'L0_ffn_w1': _L0_ffn_in['w1'], 'L0_ffn_w2': _L0_ffn_in['w2'], 'L0_ffn_w3': _L0_ffn_in['w3'], 'L0_ffn_sw1': _L0_ffn_in['sw1'], 'L0_ffn_sw2': _L0_ffn_in['sw2'], 'L0_ffn_sw3': _L0_ffn_in['sw3'], 'L0_c': _L0_c, 'L0_wmod': _L0_wmod}
    _x0 = _d['L0_attn_x']
    _d['L0_attn_x'] = jax.random.normal(jax.random.fold_in(jax.random.key(seed), 1), (8, 256, 128), dtype=_x0.dtype)
    del _x0
    return _d

def reference(L0_attn_x, L0_attn_W_dq, L0_attn_W_uq, L0_attn_W_dkv, L0_attn_W_uk, L0_attn_W_uv, L0_attn_W_o, L0_ffn_router_w, L0_ffn_expert_bias, L0_ffn_w1, L0_ffn_w2, L0_ffn_w3, L0_ffn_sw1, L0_ffn_sw2, L0_ffn_sw3, L0_c, L0_wmod):

    def _L0_attn_ref(x, W_dq, W_uq, W_dkv, W_uk, W_uv, W_o):
        import math
        import jax, jax.numpy as jnp
        import numpy as np
        N_HEAD = 16

        def _reference_tuple_inner(x, W_dq, W_uq, W_dkv, W_uk, W_uv, W_o):
            B, T, C = x.shape
            nh = N_HEAD
            hs = C // nh
            kvl = W_dkv.shape[0]
            k_eff = (W_dq.T @ W_uq.T @ W_uk).reshape(nh, hs, kvl)
            v_eff = (W_uv.T @ W_o.T).reshape(kvl, nh, hs).transpose(1, 0, 2)
            c_kv = x @ W_dkv.T
            q = (x @ W_dq.T @ W_uq.T).reshape(B, T, nh, hs).transpose(0, 2, 1, 3)
            q_lat = jnp.einsum('bhtd,hdl->bhtl', q, k_eff)
            attn = jnp.einsum('bhtl,bsl->bhts', q_lat, c_kv) / math.sqrt(hs)
            causal_mask = jnp.triu(jnp.ones((T, T), bool), k=1)
            attn = jnp.where(causal_mask[None, None], -jnp.inf, attn)
            attn = jax.nn.softmax(attn, axis=-1)
            ctx = jnp.einsum('bhts,bsl->bhtl', attn, c_kv)
            y = jnp.einsum('bhtl,hld->bhtd', ctx, v_eff).transpose(0, 2, 1, 3).reshape(B, T, C)
            return (y, c_kv)
        return _reference_tuple_inner(x, W_dq, W_uq, W_dkv, W_uk, W_uv, W_o)[0]

    def _L0_ffn_ref(x, router_w, expert_bias, w1, w2, w3, sw1, sw2, sw3):
        import jax, jax.numpy as jnp
        import numpy as np
        NUM_EXPERTS = 8
        TOP_K = 2

        def _swiglu(x, w1, w2, w3):
            return jax.nn.silu(x @ w1) * (x @ w3) @ w2
        B, S, D = x.shape
        E, K = (NUM_EXPERTS, TOP_K)
        N = B * S
        x_flat = x.reshape(N, D)
        logits = x_flat @ router_w
        scores = jax.nn.softmax(logits.astype(jnp.float32), axis=-1)
        _, sel = jax.lax.top_k(scores + expert_bias[None, :], K)
        top_scores = jnp.take_along_axis(scores, sel, axis=-1)
        flat_exp = sel.reshape(-1)
        order = jnp.argsort(flat_exp)
        exp_sorted = flat_exp[order]
        routed_input = x_flat[order // K]
        routed_output = jnp.zeros_like(routed_input)
        for e in range(E):
            mask = (exp_sorted == e)[:, None]
            y_e = _swiglu(routed_input, w1[e], w2[e], w3[e])
            routed_output = routed_output + jnp.where(mask, y_e, 0.0)
        unsorted = jnp.zeros((N * K, D), routed_output.dtype).at[order].set(routed_output)
        unsorted = unsorted.reshape(N, K, D)
        out_experts = jnp.einsum('nk,nkd->nd', top_scores, unsorted)
        shared_out = _swiglu(x_flat, sw1, sw2, sw3)
        return (shared_out + out_experts).reshape(B, S, D)
    x = L0_attn_x
    mod = (_silu(L0_c) @ L0_wmod).reshape(L0_c.shape[0], 6, 1, -1)
    sa, ca, ga, sb, cb, gb = (mod[:, 0], mod[:, 1], mod[:, 2], mod[:, 3], mod[:, 4], mod[:, 5])
    ga = (2 * (ga >= 0) - 1) * jnp.maximum(jnp.abs(ga), 0.25)
    gb = (2 * (gb >= 0) - 1) * jnp.maximum(jnp.abs(gb), 0.25)
    h = _layernorm(x, axis=-1) * (1 + ca) + sa
    x = x + ga * _L0_attn_ref(h, L0_attn_W_dq, L0_attn_W_uq, L0_attn_W_dkv, L0_attn_W_uk, L0_attn_W_uv, L0_attn_W_o)
    h = _layernorm(x, axis=-1) * (1 + cb) + sb
    x = x + gb * _L0_ffn_ref(h, L0_ffn_router_w, L0_ffn_expert_bias, L0_ffn_w1, L0_ffn_w2, L0_ffn_w3, L0_ffn_sw1, L0_ffn_sw2, L0_ffn_sw3)
    return x

_drawn_inputs = setup_inputs


def setup_inputs(seed=0):
    import zlib

    import numpy as np

    out = dict(_drawn_inputs(seed))
    spreads = {'L0_ffn_expert_bias': (0.0, 0.8)}
    factors = {'L0_attn_W_dq': 8.0,
     'L0_attn_W_uq': 8.0,
     'L0_attn_W_dkv': 8.0,
     'L0_attn_W_uk': 8.0,
     'L0_attn_W_uv': 8.0,
     'L0_attn_W_o': 8.0,
     'L0_ffn_router_w': 8.0,
     'L0_ffn_w1': 8.0,
     'L0_ffn_w2': 8.0,
     'L0_ffn_w3': 8.0,
     'L0_ffn_sw1': 8.0,
     'L0_ffn_sw2': 8.0,
     'L0_ffn_sw3': 8.0,
     'L0_c': 8.0,
     'L0_wmod': 8.0}
    for name, (base, spread) in spreads.items():
        noise = np.random.default_rng([zlib.crc32(name.encode()), seed]).standard_normal(out[name].shape)
        drawn = base * np.exp(spread * noise) if base else spread * noise
        out[name] = jnp.asarray(drawn.astype(out[name].dtype))
    for name, factor in factors.items():
        out[name] = (out[name] * factor).astype(out[name].dtype)
    return out
```

```python
import concourse.bass as bass
import concourse.mybir as mybir
from contextlib import ExitStack

F32 = mybir.dt.float32
BF16 = mybir.dt.bfloat16
ALU = mybir.AluOpType
ACT = mybir.ActivationFunctionType
AX = mybir.AxisListType

B, T, C = 8, 256, 128
NH, HS = 16, 8
E, X = 8, 9
TI = T // 128
PARTS = 3
ROWS = PARTS * PARTS * HS
MROWS = ROWS + PARTS
SPAN = NH * T
RING = 4
UNITS = 12
GROUPS = NH // 4
SCALE = float(HS) ** -0.5
EPS = 1e-5
MASKED = -1.0e38
STEPS = 12
FIRST, LAST = -2, B
STEADY = range(2, B - 2)
DMA = 16


def at(b, per, k=0):
    return b * per + k + 1


def wait(eng, sem, value):
    if not (isinstance(value, int) and value <= 0):
        eng.wait_ge(sem, value)


def alone(eng):
    eng.nop(nofuse=True)


def cols(b, width, start=0, n=None):
    return bass.ds(b * width + start, width if n is None else n)


def ring(b, start=0, n=SPAN):
    return bass.ds((b % RING) * SPAN + start, n)


def over_slots(eng, slot):
    def stages(t):
        return [0 <= t + d < B for d in (2, 1, 0, -1)]
    for t in range(FIRST, STEADY.start):
        slot(t, *stages(t))
    with eng.Fori(STEADY.start, STEADY.stop) as t:
        slot(t, True, True, True, True)
    for t in range(STEADY.stop, LAST + 1):
        slot(t, *stages(t))


def build(nc, x, W_dq, W_uq, W_dkv, W_uk, W_uv, W_o, router_w, expert_bias,
          w1, w2, w3, sw1, sw2, sw3, c, wmod, out):
    ctx = ExitStack()
    with ctx:
        def sb(name, shape, dt=F32):
            return ctx.enter_context(nc.sbuf_tensor(name, shape, dt))

        def sem(name):
            return ctx.enter_context(nc.semaphore(name))

        qk_dram = nc.dram_tensor("qk_parts", (B, 2, PARTS, HS, NH, T), BF16, kind="Internal").ap()
        mx_dram = nc.dram_tensor("max_parts", (B, PARTS * NH * TI, 128), BF16, kind="Internal").ap()

        ident = sb("ident", [128, 128])
        ident_bf = sb("ident_bf", [128, 128], BF16)
        causal = sb("causal", [128, 4, 128], BF16)
        ones_rows = sb("ones_rows", [PARTS, SPAN], BF16)
        neg_half = sb("neg_half", [128, TI])
        earlier = sb("earlier", [128, E, E])
        wdq = sb("wdq", [32, C]); wuq = sb("wuq", [C, 32]); wdkv = sb("wdkv", [32, C])
        wuk = sb("wuk", [C, 32]); wuv = sb("wuv", [C, 32]); wo = sb("wo", [C, C])
        wuqT = sb("wuqT", [32, C]); woT = sb("woT", [C, C])
        w_qT = sb("w_qT", [C, C]); w_q = sb("w_q", [C, C]); v_eff = sb("v_eff", [32, C])
        k_effT = sb("k_effT", [32, C]); w_kT = sb("w_kT", [C, C]); w_vT = sb("w_vT", [C, C])
        c_sb = sb("c_sb", [B, C]); cT = sb("cT", [C, B]); c_tanh = sb("c_tanh", [C, B])
        c_sig = sb("c_sig", [C, B]); c_silu = sb("c_silu", [C, B]); c_wide = sb("c_wide", [C, B, C])
        wm = sb("wm", [C, 6 * C])
        mod = sb("mod", [C, 4, B])
        gate_att = sb("gate_att", [128, B * C])
        gate_ffn = sb("gate_ffn", [128, B * C])
        router = sb("router", [C, E]); bias = sb("bias", [128, E])
        w_up = sb("w_up", [C, X, 2, C]); w_down = sb("w_down", [C, X, C])
        x_sb = sb("x_sb", [128, B * TI * C]); x2_sb = sb("x2_sb", [128, B * TI * C])
        v_sb = sb("v_sb", [128, B * TI * C])
        q_stack = sb("q_stack", [MROWS, RING * SPAN], BF16)
        k_stack = sb("k_stack", [MROWS, RING * SPAN], BF16)
        stats = [sb(f"stats{n}", [128, TI, 6]) for n in (1, 2)]
        mean_var = [sb(f"mean_var{n}", [128, TI, 2]) for n in (1, 2)]
        var_eps = [sb(f"var_eps{n}", [128, TI]) for n in (1, 2)]
        rstd = [sb(f"rstd{n}", [128, TI]) for n in (1, 2)]
        xn = [sb(f"xn{n}", [128, TI, C]) for n in (1, 2)]
        hT = sb("hT", [C, T]); h2T = sb("h2T", [C, T])
        qk_parts = sb("qk_parts_sb", [128, PARTS, 2, T], BF16)
        qk_rest = sb("qk_rest", [128, 2, T])
        mx = sb("mx", [128, NH, TI])
        mx_parts = sb("mx_parts_sb", [128, PARTS, NH * TI], BF16)
        mx_rest = sb("mx_rest", [128, 2, NH * TI])
        mx_rows = sb("mx_rows", [PARTS * NH * TI, 128], BF16)
        probs = sb("probs", [128, 6, 512])
        v_ones = sb("v_ones", [128, TI, NH, 32])
        yT = sb("yT", [128, 2, T])
        y_rec = sb("y_rec", [128, TI, 4]); y = sb("y", [128, TI, NH, HS])
        y_gated = sb("y_gated", [128, TI, C])
        r_max = sb("r_max", [128, TI]); r_in = sb("r_in", [128, TI, E]); r_exp = sb("r_exp", [128, TI, E])
        r_sum = sb("r_sum", [128, TI]); r_rec = sb("r_rec", [128, TI]); score = sb("score", [128, TI, E])
        biased = sb("biased", [128, TI, E]); above = sb("above", [128, TI, E, E])
        ahead = sb("ahead", [128, TI, E, E])
        equal = sb("equal", [128, TI, E, E]); rank = sb("rank", [128, TI, E]); gates = sb("gates", [128, TI, E])
        gates_wide = sb("gates_wide", [128, E, T])
        g_sign, g_neg, g_abs = probs[:, 0, :], probs[:, 1, :], probs[:, 2, :]
        g_tanh = sb("g_tanh", [128, 2, T]); act_g = sb("act_g", [128, 2, T]); hidden = sb("hidden", [128, 2, T])
        f_out = sb("f_out", [128, TI, C]); o_sb = sb("o_sb", [128, TI, C])

        bank = [ctx.enter_context(nc.psum_tensor(f"bank{i}", [128, 512], F32)) for i in range(8)]
        P_MAX, P_EXP, P_UP, P_ACC, P_FRONT, P_BACK = bank[0], bank[1:3], bank[3:5], bank[5], bank[6], bank[7]

        names = """ld_small ld_c ld_x ld_up ld_down ld_ones k_ident k_mask k_rest k_fill
            t_setup e_setup t_gate e_gate m_tanh m_sig m_silu m_wide gs_step ga_done
            ln1_stats ln1_mv ln1_ve ln1_rstd ln1_norm xT_ready hT_ready qk_ready part1 rest1 part2 part3
            v_ready v_saved qk_stored stacked s1_ready s1_max m_part1 m_rest1 m_part2 m_rest2 m_part3
            mT_ready mT_saved m_stored m_stacked
            v_placed s2_ready s2_exp s2_masked pv_ready yT_saved ytr_ready y_recip y_norm y_gate x2_ready
            ln2_stats ln2_mv ln2_ve ln2_rstd ln2_norm h2x_ready h2T_ready r_ready r_maxed r_shifted r_exped
            r_summed r_inv r_score r_biased r_ahead r_above r_equal r_tied r_counted r_ranked gates_ready
            gw_ready gw_saved up_ready tanhed silued gated hid_ready down_ready f_gated o_ready stored"""
        S = {n: sem(n) for n in names.split()}
        block = ctx.enter_context(nc.Block())
        N_SETUP = 4

        @block.sync
        def _(sp):
            for dst, src in ((wuq, W_uq), (wo, W_o), (wdq, W_dq), (wuk, W_uk), (wuv, W_uv), (wdkv, W_dkv)):
                sp.dma_start(dst[:], src).then_inc(S["ld_small"], DMA)
            sp.dma_start(w_up[:, 0:E, 0, :], w1.rearrange("e d h -> d e h")).then_inc(S["ld_up"], DMA)
            sp.dma_start(w_up[:, 0:E, 1, :], w3.rearrange("e d h -> d e h")).then_inc(S["ld_up"], DMA)
            sp.dma_start(w_up[:, E, 0, :], sw1).then_inc(S["ld_up"], DMA)
            sp.dma_start(w_up[:, E, 1, :], sw3).then_inc(S["ld_up"], DMA)
            sp.dma_start(w_down[:, 0:E, :], w2.rearrange("e h d -> h e d")).then_inc(S["ld_down"], DMA)
            sp.dma_start(w_down[:, E, :], sw2).then_inc(S["ld_down"], DMA)
            sp.wait_ge(S["k_fill"], 1)
            for b in range(RING):
                sp.dma_start(k_stack[ROWS:MROWS, b * SPAN:(b + 1) * SPAN], ones_rows[:, :]).then_inc(S["ld_ones"], DMA)

            def slot(t, A, Bs, Cs, D):
                if A:
                    b = t + 2
                    sp.wait_ge(S["part3"], at(b, 1))
                    for s in range(2):
                        for i in range(PARTS):
                            sp.dma_start(qk_dram[bass.ds(b, 1), s, i].rearrange("b d h t -> b h d t")[0],
                                         qk_parts[:, i, s, :]).then_inc(S["qk_stored"], DMA)
                    sp.wait_ge(S["qk_stored"], b * 6 * DMA + 6 * DMA)
                    wait(sp, S["s2_ready"], (b - RING + 1) * UNITS)
                    for i in range(PARTS):
                        src = qk_dram[bass.ds(b, 1), 0, i].rearrange("b d h t -> (b d) (h t)")
                        sp.dma_start(q_stack[24 * i:24 * i + 24, ring(b)],
                                     src.unsqueeze(0).to_broadcast([PARTS, HS, SPAN])).then_inc(S["stacked"], DMA)
                    src = qk_dram[bass.ds(b, 1), 1].rearrange("b i d h t -> (b i d) (h t)")
                    sp.dma_start(k_stack[0:ROWS, ring(b)],
                                 src.unsqueeze(0).to_broadcast([PARTS, PARTS * HS, SPAN])).then_inc(S["stacked"], DMA)
                if Bs:
                    b = t + 1
                    sp.wait_ge(S["mT_saved"], at(b, 1))
                    sp.dma_start(mx_dram[bass.ds(b, 1)].rearrange("b r q -> (b r) q"), mx_rows[:, :])\
                      .then_inc(S["m_stored"], DMA)
                    sp.wait_ge(S["m_stored"], b * DMA + DMA)
                    sp.dma_start(q_stack[ROWS:MROWS, ring(b)],
                                 mx_dram[bass.ds(b, 1)].rearrange("b (i r) q -> (b i) (r q)", i=PARTS))\
                      .then_inc(S["m_stacked"], DMA)
                if D:
                    b = t - 1
                    sp.wait_ge(S["o_ready"], at(b, 1))
                    sp.dma_start(out[bass.ds(b, 1)].rearrange("b (i p) c -> p (b i) c", p=128), o_sb[:, :, :])\
                      .then_inc(S["stored"], DMA)
            over_slots(sp, slot)
            sp.wait_ge(S["stored"], B * DMA)

        @block.gpsimd
        def _(pool):
            g = nc.gpsimd
            g.memset(ident[:], 0.0).then_inc(S["k_ident"], 1)
            g.memset(ident_bf[:], 0.0).then_inc(S["k_ident"], 1)
            pool.wait_ge(S["k_ident"], 2)
            for m in (ident, ident_bf):
                g.affine_select(out=m[:], in_=m[:], compare_op=ALU.not_equal, fill=1.0, base=0,
                                pattern=[[-1, 128]], channel_multiplier=1).then_inc(S["k_ident"], 1)
            g.memset(ones_rows[:], 1.0).then_inc(S["k_fill"], 1)
            g.memset(neg_half[:], -0.5).then_inc(S["k_rest"], 1)
            g.memset(causal[:], 0.0).then_inc(S["k_mask"], 1)
            g.memset(earlier[:], 1.0).then_inc(S["k_rest"], 1)
            g.memset(v_ones[:], 0.0).then_inc(S["k_rest"], 1)
            pool.wait_ge(S["k_mask"], 1)
            g.affine_select(out=causal[:], in_=causal[:], compare_op=ALU.is_ge, fill=MASKED, base=0,
                            pattern=[[0, 4], [-1, 128]], channel_multiplier=1).then_inc(S["k_mask"], 1)
            pool.wait_ge(S["k_rest"], 3)
            g.affine_select(out=earlier[:], in_=earlier[:], compare_op=ALU.is_gt, fill=0.0, base=0,
                            pattern=[[1, E], [-1, E]], channel_multiplier=0).then_inc(S["k_rest"], 1)
            g.memset(v_ones[:, :, :, HS], 1.0).then_inc(S["k_rest"], 1)
            pool.wait_ge(S["k_rest"], 5)

            def inv_std(n, b):
                pool.wait_ge(S[f"ln{n}_mv"], at(b, 1))
                alone(pool)
                g.tensor_scalar(var_eps[n - 1][:], mean_var[n - 1][:, :, 1], EPS, None, ALU.add)\
                 .then_inc(S[f"ln{n}_ve"], 1)
                pool.wait_ge(S[f"ln{n}_ve"], at(b, 1))
                wait(pool, S[f"ln{n}_norm"], b)
                g.tensor_tensor(rstd[n - 1][:], var_eps[n - 1][:], neg_half[:], ALU.pow)\
                 .then_inc(S[f"ln{n}_rstd"], 1)

            def mask(b, u):
                pool.wait_ge(S["s2_exp"], at(b, UNITS, u))
                alone(pool)
                buf = probs[:, u % 6, :]
                v = buf.rearrange("k (h q) -> k h q", h=4) if u % 3 == 2 else \
                    buf.rearrange("k (h q) -> k h q", h=2)[:, :, 0:128]
                g.affine_select(out=v, in_=v, compare_op=ALU.is_ge, fill=0.0, base=0,
                                pattern=[[0, 4 if u % 3 == 2 else 2], [1, 128]], channel_multiplier=-1)\
                 .then_inc(S["s2_masked"], 1)

            def slot(t, A, Bs, Cs, D):
                if Cs:
                    pool.wait_ge(S["v_saved"], at(t, 1))
                    wait(pool, S["pv_ready"], t * GROUPS)
                    alone(pool)
                    g.tensor_copy(v_ones[:, :, :, 0:HS],
                                  v_sb[:, cols(t, TI * C)].rearrange("p (i h d) -> p i h d", i=TI, h=NH))\
                     .then_inc(S["v_placed"], 1)
                for s in range(STEPS):
                    if Cs and s < 6:
                        mask(t, 2 * s)
                    if D and 1 <= s < X:
                        b = t - 1
                        pool.wait_ge(S["silued"], at(b, X, s))
                        pool.wait_ge(S["gw_saved"], at(b, 4, (s - 1) // 2))
                        g.tensor_tensor(act_g[:, s % 2, :], act_g[:, s % 2, :], gates_wide[:, s - 1, :], ALU.mult)\
                         .then_inc(S["gated"], 1)
                    if Cs and s < 6:
                        mask(t, 2 * s + 1)
                    if A and s == 2:
                        inv_std(1, t + 2)
                    if A and s == 6:
                        b = t + 2
                        pool.wait_ge(S["rest1"], at(b, 1))
                        wait(pool, S["qk_stored"], b * 6 * DMA)
                        alone(pool)
                        g.tensor_copy(qk_parts[:, 1], qk_rest[:]).then_inc(S["part2"], 1)
                        pool.wait_ge(S["part2"], at(b, 1))
                        g.tensor_tensor(qk_parts[:, 2], qk_rest[:], qk_parts[:, 1], ALU.subtract)\
                         .then_inc(S["part3"], 1)
                    if Bs and s == 7:
                        b = t + 1
                        m = mx[:].rearrange("p h i -> p (h i)")
                        pool.wait_ge(S["s1_max"], at(b, UNITS, UNITS - 1))
                        wait(pool, S["mT_ready"], b)
                        alone(pool)
                        g.tensor_scalar(mx_parts[:, 0], m, -1.0, None, ALU.mult).then_inc(S["m_part1"], 1)
                        pool.wait_ge(S["m_part1"], at(b, 1))
                        g.tensor_tensor(mx_rest[:, 0], m, mx_parts[:, 0], ALU.add).then_inc(S["m_rest1"], 1)
                        pool.wait_ge(S["m_rest1"], at(b, 1))
                        alone(pool)
                        g.tensor_scalar(mx_parts[:, 1], mx_rest[:, 0], -1.0, None, ALU.mult)\
                         .then_inc(S["m_part2"], 1)
                        pool.wait_ge(S["m_part2"], at(b, 1))
                        g.tensor_tensor(mx_rest[:, 1], mx_rest[:, 0], mx_parts[:, 1], ALU.add)\
                         .then_inc(S["m_rest2"], 1)
                        pool.wait_ge(S["m_rest2"], at(b, 1))
                        alone(pool)
                        g.tensor_scalar(mx_parts[:, 2], mx_rest[:, 1], -1.0, None, ALU.mult)\
                         .then_inc(S["m_part3"], 1)
                    if Cs and s == 8:
                        inv_std(2, t)
                    if Cs and s == 11:
                        pool.wait_ge(S["r_inv"], at(t, 1))
                        wait(pool, S["gates_ready"], t)
                        g.tensor_tensor(score[:], r_exp[:], r_rec[:].unsqueeze(2).to_broadcast([128, TI, E]),
                                        ALU.mult).then_inc(S["r_score"], 1)
                        pool.wait_ge(S["r_score"], at(t, 1))
                        g.tensor_tensor(biased[:], score[:], bias[:].unsqueeze(1).to_broadcast([128, TI, E]),
                                        ALU.add).then_inc(S["r_biased"], 1)
                        pool.wait_ge(S["r_biased"], at(t, 1))
                        wait(pool, S["r_ranked"], t)
                        for i in range(TI):
                            other = biased[:, i].unsqueeze(1).to_broadcast([128, E, E])
                            own = biased[:, i].unsqueeze(2).to_broadcast([128, E, E])
                            g.tensor_tensor(ahead[:, i], other, own, ALU.subtract).then_inc(S["r_ahead"], 1)
                        pool.wait_ge(S["r_ahead"], at(t, TI, TI - 1))
                        alone(pool)
                        g.tensor_scalar(equal[:], ahead[:], 0.0, None, ALU.is_equal).then_inc(S["r_equal"], 1)
                        g.tensor_scalar(above[:], ahead[:], 0.0, None, ALU.is_gt).then_inc(S["r_above"], 1)
                        pool.wait_ge(S["r_equal"], at(t, 1))
                        for i in range(TI):
                            g.tensor_tensor(equal[:, i], equal[:, i], earlier[:], ALU.mult)\
                             .then_inc(S["r_tied"], 1)
                        pool.wait_ge(S["r_tied"], at(t, TI, TI - 1))
                        pool.wait_ge(S["r_above"], at(t, 1))
                        g.tensor_tensor(above[:], above[:], equal[:], ALU.add).then_inc(S["r_counted"], 1)

            pool.wait_ge(S["ld_c"], 4 * DMA)
            over_slots(pool, slot)

        @block.scalar
        def _(act):
            a = nc.scalar
            act.dma_start(c_sb[:], c).then_inc(S["ld_c"], DMA)
            act.dma_start(wm[:], wmod).then_inc(S["ld_c"], DMA)
            for n in range(4):
                k = B * TI // 4
                act.dma_start(x_sb[:, n * k * C:(n + 1) * k * C].rearrange("p (i c) -> p i c", c=C),
                              x.rearrange("b (i p) c -> p (b i) c", p=128)[:, n * k:(n + 1) * k, :])\
                   .then_inc(S["ld_x"], DMA)
            act.dma_start(router[:], router_w).then_inc(S["ld_c"], DMA)
            act.dma_start(bias[:], expert_bias.unsqueeze(0).to_broadcast([128, E])).then_inc(S["ld_c"], DMA)
            act.wait_ge(S["e_setup"], 1)
            a.activation(c_tanh[:], cT[:], ACT.Tanh, scale=0.5).then_inc(S["m_tanh"], 1)

            def exps(b, u):
                act.wait_ge(S["s2_ready"], at(b, UNITS, u))
                wait(act, S["pv_ready"], at(b, GROUPS, (u - 6) // 3))
                a.activation(probs[:, u % 6, :], P_EXP[u % 2][:], ACT.Exp, scale=SCALE).then_inc(S["s2_exp"], 1)

            def slot(t, A, Bs, Cs, D):
                for s in range(STEPS):
                    if Cs and s < 6:
                        exps(t, 2 * s)
                    if D and s < X:
                        b = t - 1
                        act.wait_ge(S["up_ready"], at(b, X, s))
                        wait(act, S["silued"], at(b, X, s - 2))
                        a.activation(g_tanh[:, s % 2, :], P_UP[s % 2][:, 0:T], ACT.Tanh, scale=0.5)\
                         .then_inc(S["tanhed"], 1)
                    if D and 1 <= s < 5:
                        b = t - 1
                        act.wait_ge(S["gw_ready"], at(b, 4, s - 1))
                        wait(act, S["gated"], b * E)
                        a.activation(gates_wide[:, 2 * s - 2:2 * s, :],
                                     P_FRONT[:].rearrange("p (e t) -> p e t", e=2), ACT.Copy)\
                         .then_inc(S["gw_saved"], 1)
                    if Cs and s < 6:
                        exps(t, 2 * s + 1)
                    if Cs and s in (2, 3, 5, 6):
                        g = (2, 3, 5, 6).index(s)
                        act.wait_ge(S["pv_ready"], at(t, GROUPS, g))
                        wait(act, S["ytr_ready"], at(t, GROUPS, g - 2))
                        a.activation(yT[:, g % 2, :], P_BACK[:, 0:T], ACT.Copy).then_inc(S["yT_saved"], 1)
                    if A and s == 5:
                        b = t + 2
                        act.wait_ge(S["xT_ready"], at(b, 1))
                        wait(act, S["v_ready"], b)
                        a.activation(hT[:], P_FRONT[:, 0:T], ACT.Identity, bias=mod[:, 0, bass.ds(b, 1)],
                                     scale=mod[:, 1, bass.ds(b, 1)]).then_inc(S["hT_ready"], 1)
                    if A and s == 6:
                        b = t + 2
                        act.wait_ge(S["qk_ready"], at(b, 1))
                        wait(act, S["qk_stored"], b * 6 * DMA)
                        a.activation(qk_parts[:, 0], P_FRONT[:].rearrange("p (s t) -> p s t", s=2), ACT.Copy)\
                         .then_inc(S["part1"], 1)
                    if Bs and s == 8:
                        b = t + 1
                        act.wait_ge(S["mT_ready"], at(b, 1))
                        wait(act, S["m_stored"], b * DMA)
                        a.activation(mx_rows[:], P_FRONT[0:96, 0:64].bitcast(BF16), ACT.Copy)\
                         .then_inc(S["mT_saved"], 1)
                    if Cs and s == 10:
                        act.wait_ge(S["h2x_ready"], at(t, 1))
                        wait(act, S["up_ready"], t * X)
                        a.activation(h2T[:], P_BACK[:, 0:T], ACT.Identity, bias=mod[:, 2, bass.ds(t, 1)],
                                     scale=mod[:, 3, bass.ds(t, 1)]).then_inc(S["h2T_ready"], 1)
                    if Cs and s == 11:
                        act.wait_ge(S["r_shifted"], at(t, 1))
                        wait(act, S["r_score"], t)
                        a.activation(r_exp[:], r_in[:], ACT.Exp).then_inc(S["r_exped"], 1)
            act.wait_ge(S["e_setup"], N_SETUP + 1)
            over_slots(act, slot)

        @block.vector
        def _(dve):
            v = nc.vector
            dve.wait_ge(S["t_setup"], 1)
            v.tensor_copy(cT[:], bank[0][:, 0:B])
            v.tensor_copy(wuqT[:], bank[0][0:32, 128:256])
            v.tensor_copy(woT[:], bank[0][:, 256:384]).then_inc(S["e_setup"], 1)
            dve.wait_ge(S["t_setup"], 2)
            v.tensor_copy(w_qT[:], bank[1][:, 0:128])
            v.tensor_copy(w_q[:], bank[1][:, 128:256])
            v.tensor_copy(v_eff[:], bank[1][0:32, 256:384]).then_inc(S["e_setup"], 1)
            dve.wait_ge(S["t_setup"], 3)
            v.tensor_copy(k_effT[:], bank[2][0:32, 0:128]).then_inc(S["e_setup"], 1)
            dve.wait_ge(S["m_tanh"], 1)
            v.tensor_scalar(c_sig[:], c_tanh[:], 1.0, 0.5, ALU.add, ALU.mult).then_inc(S["m_sig"], 1)
            dve.wait_ge(S["m_sig"], 1)
            v.tensor_tensor(c_silu[:], c_sig[:], cT[:], ALU.mult).then_inc(S["m_silu"], 1)
            dve.wait_ge(S["t_setup"], 4)
            v.tensor_copy(w_kT[:], bank[3][:, 0:128])
            v.tensor_copy(w_vT[:], bank[3][:, 128:256]).then_inc(S["e_setup"], 1)
            dve.wait_ge(S["m_silu"], 1)
            v.tensor_copy(c_wide[:], c_silu[:].unsqueeze(2).to_broadcast([C, B, C])).then_inc(S["m_wide"], 1)
            dve.wait_ge(S["t_setup"], 5)
            for n, plus in enumerate((0.0, 1.0, 0.0, 1.0)):
                last = v.tensor_scalar(mod[:, n], bank[4][:, n * B:n * B + B], plus, None, ALU.add)
            last.then_inc(S["e_setup"], 1)

            def gate_tables():
                for n in range(4):
                    half = n % 2
                    dst = (gate_att if n < 2 else gate_ffn)[:, half * 512:half * 512 + 512]
                    f = 1.0 if n < 2 else 0.5
                    dve.wait_ge(S["t_gate"], n + 1)
                    wait(dve, S["ga_done"], n)
                    v.tensor_scalar(g_sign, bank[(3, 4, 5, 7)[n]][:], 0.0, 2.0 * f, ALU.is_ge, ALU.mult)
                    v.tensor_scalar(g_neg, bank[(3, 4, 5, 7)[n]][:], -1.0, None, ALU.mult)\
                     .then_inc(S["gs_step"], 1)
                    dve.wait_ge(S["gs_step"], 2 * n + 1)
                    v.scalar_tensor_tensor(g_abs, g_neg, 0.25, bank[(3, 4, 5, 7)[n]][:], ALU.max, ALU.max)\
                     .then_inc(S["gs_step"], 1)
                    dve.wait_ge(S["gs_step"], 2 * n + 2)
                    v.scalar_tensor_tensor(dst, g_sign, -f, g_abs, ALU.add, ALU.mult)\
                     .then_inc(S["ga_done"], 1)

            def ln_stats(n, b, src):
                wait(dve, S[f"ln{n}_norm"], b)
                alone(dve)
                for i in range(TI):
                    last = v.bn_stats(stats[n - 1][:, i], src[:, cols(b, TI * C, i * C, C)])
                last.then_inc(S[f"ln{n}_stats"], 1)
                dve.wait_ge(S[f"ln{n}_stats"], at(b, 1))
                alone(dve)
                for i in range(TI):
                    last = v.bn_aggr(mean_var[n - 1][:, i], stats[n - 1][:, i])
                last.then_inc(S[f"ln{n}_mv"], 1)

            def ln_norm(n, b, src, used):
                dve.wait_ge(S[f"ln{n}_rstd"], at(b, 1))
                wait(dve, S[used], b)
                for i in range(TI):
                    last = v.tensor_scalar(xn[n - 1][:, i], src[:, cols(b, TI * C, i * C, C)],
                                           mean_var[n - 1][:, i, 0:1], rstd[n - 1][:, i:i + 1],
                                           ALU.subtract, ALU.mult)
                last.then_inc(S[f"ln{n}_norm"], 1)

            def row_max(b, u):
                dve.wait_ge(S["s1_ready"], at(b, UNITS, u))
                if u == 0:
                    wait(dve, S["m_part3"], b)
                if u < 4:
                    dst, n = mx[:, 4 * u:4 * u + 4, 0], 4
                else:
                    dst, n = mx[:, 2 * (u - 4):2 * (u - 4) + 2, 1], 2
                v.tensor_reduce(dst, P_MAX[:].rearrange("p (h k) -> p h k", h=n), AX.X, ALU.max)\
                 .then_inc(S["s1_max"], 1)

            def hidden_of(b, n):
                if n == 0:
                    dve.wait_ge(S["silued"], at(b, X, 0))
                else:
                    dve.wait_ge(S["gated"], at(b, E, n - 1))
                wait(dve, S["down_ready"], at(b, X, n - 2))
                v.tensor_tensor(hidden[:, n % 2, :], P_UP[n % 2][:, T:2 * T], act_g[:, n % 2, :], ALU.mult)\
                 .then_inc(S["hid_ready"], 1)

            def slot(t, A, Bs, Cs, D):
                for s in range(STEPS):
                    if Bs and s < 6:
                        row_max(t + 1, 2 * s)
                    if D and s < X:
                        b = t - 1
                        dve.wait_ge(S["tanhed"], at(b, X, s))
                        wait(dve, S["hid_ready"], at(b, X, s - 2))
                        v.scalar_tensor_tensor(act_g[:, s % 2, :], g_tanh[:, s % 2, :], 1.0,
                                               P_UP[s % 2][:, 0:T], ALU.add, ALU.mult)\
                         .then_inc(S["silued"], 1)
                    if Bs and s < 6:
                        row_max(t + 1, 2 * s + 1)
                    if D and s == 0:
                        b = t - 1
                        dve.wait_ge(S["r_counted"], at(b, 1))
                        v.tensor_reduce(rank[:], above[:], AX.X, ALU.add).then_inc(S["r_ranked"], 1)
                        dve.wait_ge(S["r_ranked"], at(b, 1))
                        wait(dve, S["gw_ready"], b * 4)
                        v.scalar_tensor_tensor(gates[:], rank[:], 1.5, score[:], ALU.is_lt, ALU.mult)\
                         .then_inc(S["gates_ready"], 1)
                    if D and 1 <= s <= X:
                        hidden_of(t - 1, s - 1)
                    if A and s == 2:
                        b = t + 2
                        dve.wait_ge(S["ld_x"], 4 * DMA)
                        ln_stats(1, b, x_sb)
                    if A and s == 3:
                        ln_norm(1, t + 2, x_sb, "xT_ready")
                    if Cs and s in (3, 4, 6, 7):
                        g = (3, 4, 6, 7).index(s)
                        src = P_BACK[:, 0:T].rearrange("p (i h r) -> p i h r", i=TI, h=4)
                        dve.wait_ge(S["ytr_ready"], at(t, GROUPS, g))
                        wait(dve, S["y_norm"], at(t, GROUPS, g - 1))
                        v.reciprocal(y_rec[:], src[:, :, :, HS]).then_inc(S["y_recip"], 1)
                        dve.wait_ge(S["y_recip"], at(t, GROUPS, g))
                        if g == 0:
                            wait(dve, S["y_gate"], t)
                        v.tensor_tensor(y[:, :, 4 * g:4 * g + 4, :], src[:, :, :, 0:HS],
                                        y_rec[:].unsqueeze(3).to_broadcast([128, TI, 4, HS]), ALU.mult)\
                         .then_inc(S["y_norm"], 1)
                    if A and s == 6:
                        b = t + 2
                        dve.wait_ge(S["part1"], at(b, 1))
                        wait(dve, S["part3"], b)
                        v.tensor_tensor(qk_rest[:], P_FRONT[:].rearrange("p (s t) -> p s t", s=2),
                                        qk_parts[:, 0], ALU.subtract).then_inc(S["rest1"], 1)
                    if A and s == 7:
                        b = t + 2
                        dve.wait_ge(S["v_ready"], at(b, 1))
                        v.tensor_copy(v_sb[:, cols(b, TI * C)], P_FRONT[:, 0:TI * C]).then_inc(S["v_saved"], 1)
                    if Cs and s == 8:
                        dve.wait_ge(S["y_norm"], at(t, GROUPS, GROUPS - 1))
                        wait(dve, S["x2_ready"], t)
                        v.tensor_tensor(y_gated[:], y[:].rearrange("p i h d -> p i (h d)"),
                                        gate_att[:, cols(t, C)].unsqueeze(1).to_broadcast([128, TI, C]),
                                        ALU.mult).then_inc(S["y_gate"], 1)
                        dve.wait_ge(S["y_gate"], at(t, 1))
                        v.tensor_tensor(x2_sb[:, cols(t, TI * C)], x_sb[:, cols(t, TI * C)],
                                        y_gated[:].rearrange("p i c -> p (i c)"), ALU.add)\
                         .then_inc(S["x2_ready"], 1)
                        dve.wait_ge(S["x2_ready"], at(t, 1))
                        ln_stats(2, t, x2_sb)
                    if Cs and s == 9:
                        ln_norm(2, t, x2_sb, "h2x_ready")
                    if Cs and s == 11:
                        src = P_BACK[:, 0:TI * E].rearrange("p (i e) -> p i e", i=TI)
                        dve.wait_ge(S["r_ready"], at(t, 1))
                        v.tensor_reduce(r_max[:], src, AX.X, ALU.max).then_inc(S["r_maxed"], 1)
                        dve.wait_ge(S["r_maxed"], at(t, 1))
                        wait(dve, S["r_exped"], t)
                        v.tensor_tensor(r_in[:], src, r_max[:].unsqueeze(2).to_broadcast([128, TI, E]),
                                        ALU.subtract).then_inc(S["r_shifted"], 1)
                        dve.wait_ge(S["r_exped"], at(t, 1))
                        v.tensor_reduce(r_sum[:], r_exp[:], AX.X, ALU.add).then_inc(S["r_summed"], 1)
                        dve.wait_ge(S["r_summed"], at(t, 1))
                        wait(dve, S["r_score"], t)
                        v.reciprocal(r_rec[:], r_sum[:]).then_inc(S["r_inv"], 1)
                    if D and s == 11:
                        b = t - 1
                        dve.wait_ge(S["down_ready"], at(b, X, X - 1))
                        wait(dve, S["o_ready"], b)
                        v.tensor_tensor(f_out[:], P_ACC[:, 0:TI * C].rearrange("p (i c) -> p i c", i=TI),
                                        gate_ffn[:, cols(b, C)].unsqueeze(1).to_broadcast([128, TI, C]),
                                        ALU.mult).then_inc(S["f_gated"], 1)
                        dve.wait_ge(S["f_gated"], at(b, 1))
                        wait(dve, S["stored"], b * DMA)
                        v.tensor_tensor(o_sb[:].rearrange("p i c -> p (i c)"), f_out[:].rearrange("p i c -> p (i c)"),
                                        x2_sb[:, cols(b, TI * C)], ALU.add).then_inc(S["o_ready"], 1)
                if isinstance(t, int) and t == FIRST:
                    gate_tables()
            over_slots(dve, slot)

        @block.tensor
        def _(pe):
            mm, tr = nc.tensor.matmul, nc.tensor.transpose
            pe.wait_ge(S["k_ident"], 4)
            pe.wait_ge(S["ld_small"], 6 * DMA)
            pe.wait_ge(S["ld_c"], 4 * DMA)
            tr(bank[0][:, 0:B], c_sb[:], ident[0:B, 0:B])
            tr(bank[0][0:32, 128:256], wuq[:], ident[:])
            tr(bank[0][:, 256:384], wo[:], ident[:]).then_inc(S["t_setup"], 1)
            pe.wait_ge(S["e_setup"], 1)
            mm(bank[1][:, 0:128], wdq[:], wuqT[:], start=True, stop=True)
            mm(bank[1][:, 128:256], wuqT[:], wdq[:], start=True, stop=True)
            mm(bank[1][0:32, 256:384], wuv[:], woT[:], start=True, stop=True).then_inc(S["t_setup"], 1)
            pe.wait_ge(S["e_setup"], 2)
            mm(bank[2][0:32, 0:128], wuk[:], w_q[:], start=True, stop=True).then_inc(S["t_setup"], 1)
            pe.wait_ge(S["e_setup"], 3)
            mm(bank[3][:, 0:128], wdkv[:], k_effT[:], start=True, stop=True)
            mm(bank[3][:, 128:256], wdkv[:], v_eff[:], start=True, stop=True).then_inc(S["t_setup"], 1)
            pe.wait_ge(S["m_silu"], 1)
            for n, s in enumerate((0, 1, 3, 4)):
                last = mm(bank[4][:, n * B:n * B + B], wm[:, s * C:(s + 1) * C], c_silu[:], start=True, stop=True)
            last.then_inc(S["t_setup"], 1)
            pe.wait_ge(S["e_setup"], N_SETUP + 1)

            def gate_tables():
                pe.wait_ge(S["m_wide"], 1)
                for n in range(4):
                    s = 2 if n < 2 else 5
                    for k in range(4):
                        last = mm(bank[(3, 4, 5, 7)[n]][:, k * C:(k + 1) * C], c_wide[:, 4 * (n % 2) + k, :],
                                  wm[:, s * C:(s + 1) * C], start=True, stop=True)
                    last.then_inc(S["t_gate"], 1)

            def max_unit(b, u):
                wait(pe, S["s1_max"], b * UNITS + u)
                if u == 0:
                    pe.wait_ge(S["stacked"], b * 4 * DMA + 4 * DMA)
                if u < 4:
                    mm(P_MAX[:], ident_bf[:], causal[:].rearrange("p h k -> p (h k)"), start=True, stop=False,
                       skip_group_check=True)
                    for j in range(4):
                        h = 4 * u + j
                        last = mm(P_MAX[:, j * 128:j * 128 + 128], q_stack[0:ROWS, ring(b, h * T, 128)],
                                  k_stack[0:ROWS, ring(b, h * T, 128)], start=False, stop=(j == 3),
                                  skip_group_check=True)
                else:
                    mm(P_MAX[:].rearrange("p (h k) -> p h k", h=2)[:, :, 128:256], ident_bf[:], causal[:, 0:2, :],
                       start=True, stop=False, skip_group_check=True)
                    for j in range(2):
                        h = 2 * (u - 4) + j
                        last = mm(P_MAX[:, j * T:j * T + T], q_stack[0:ROWS, ring(b, h * T + 128, 128)],
                                  k_stack[0:ROWS, ring(b, h * T, T)], start=False, stop=(j == 1),
                                  skip_group_check=True)
                last.then_inc(S["s1_ready"], 1)

            def exp_unit(b, u):
                wait(pe, S["s2_exp"], b * UNITS + u - 1)
                if u == 0:
                    pe.wait_ge(S["m_stacked"], b * DMA + DMA)
                g, r = divmod(u, 3)
                if r < 2:
                    for j in range(2):
                        h = 4 * g + 2 * r + j
                        last = mm(P_EXP[u % 2][:, j * T:j * T + T], k_stack[:, ring(b, h * T, 128)],
                                  q_stack[:, ring(b, h * T, T)], start=True, stop=True)
                else:
                    for j in range(4):
                        h = 4 * g + j
                        last = mm(P_EXP[u % 2][:, j * 128:j * 128 + 128],
                                  k_stack[:, ring(b, h * T + 128, 128)],
                                  q_stack[:, ring(b, h * T + 128, 128)], start=True, stop=True)
                last.then_inc(S["s2_ready"], 1)

            def probs_v(b, g):
                pe.wait_ge(S["s2_masked"], at(b, UNITS, 3 * g + 2))
                if g == 0:
                    pe.wait_ge(S["v_placed"], at(b, 1))
                    wait(pe, S["r_shifted"], b)
                elif g == 2:
                    pe.wait_ge(S["y_norm"], at(b, GROUPS, 1))
                else:
                    pe.wait_ge(S["yT_saved"], at(b, GROUPS, g - 1))
                for j in range(4):
                    unit = probs[:, (3 * g + 2) % 6, :]
                    mm(P_BACK[32 * j:32 * j + 32, 128:T], v_ones[:, 1, 4 * g + j, :],
                       unit[:, j * 128:j * 128 + 128], start=True, stop=False, skip_group_check=True)
                for j in range(4):
                    unit = probs[:, (3 * g + j // 2) % 6, :]
                    last = mm(P_BACK[32 * j:32 * j + 32, 0:T], v_ones[:, 0, 4 * g + j, :],
                              unit[:, (j % 2) * T:(j % 2) * T + T], start=False, stop=True,
                              skip_group_check=True)
                last.then_inc(S["pv_ready"], 1)

            def y_back(b, g):
                pe.wait_ge(S["yT_saved"], at(b, GROUPS, g | 1))
                if g % 2:
                    pe.wait_ge(S["y_norm"], at(b, GROUPS, g - 1))
                for i in range(TI):
                    last = tr(P_BACK[:, i * 128:i * 128 + 128], yT[:, g % 2, i * 128:i * 128 + 128], ident[:])
                last.then_inc(S["ytr_ready"], 1)

            def slot(t, A, Bs, Cs, D):
                for s in range(STEPS):
                    if Cs and s < 6:
                        exp_unit(t, 2 * s)
                    if Bs and s < 6:
                        max_unit(t + 1, 2 * s)
                    if D and s < X:
                        b, e = t - 1, (s - 1) % X
                        if s == 0:
                            pe.wait_ge(S["h2T_ready"], at(b, 1))
                        wait(pe, S["hid_ready"], at(b, X, s - 2))
                        for k in range(2):
                            last = mm(P_UP[s % 2][:, k * T:k * T + T], w_up[:, e, k, :], h2T[:],
                                      start=True, stop=True)
                        last.then_inc(S["up_ready"], 1)
                    if Cs and s < 6:
                        exp_unit(t, 2 * s + 1)
                    if Bs and s < 6:
                        max_unit(t + 1, 2 * s + 1)
                    if D and 1 <= s < 5:
                        b = t - 1
                        if s == 1:
                            pe.wait_ge(S["gates_ready"], at(b, 1))
                            wait(pe, S["mT_saved"], min(t + 1, B) if isinstance(t, int) else t + 1)
                        wait(pe, S["gw_saved"], at(b, 4, s - 2))
                        for k in range(2):
                            for i in range(TI):
                                last = tr(P_FRONT[:, k * T + i * 128:k * T + i * 128 + 128],
                                          gates[:, i, 2 * (s - 1) + k:2 * (s - 1) + k + 1].to_broadcast([128, 128]),
                                          ident[:])
                        last.then_inc(S["gw_ready"], 1)
                    if A and s == 5:
                        b = t + 2
                        pe.wait_ge(S["ln1_norm"], at(b, 1))
                        wait(pe, S["v_saved"], b)
                        wait(pe, S["mT_saved"], b - 1)
                        if D:
                            pe.wait_ge(S["gw_saved"], at(t - 1, 4, 3))
                        for i in range(TI):
                            last = tr(P_FRONT[:, i * 128:i * 128 + 128], xn[0][:, i, :], ident[:])
                        last.then_inc(S["xT_ready"], 1)
                    if A and s == 6:
                        b = t + 2
                        pe.wait_ge(S["hT_ready"], at(b, 1))
                        mm(P_FRONT[:, 0:T], w_qT[:], hT[:], start=True, stop=True)
                        mm(P_FRONT[:, T:2 * T], w_kT[:], hT[:], start=True, stop=True).then_inc(S["qk_ready"], 1)
                    if A and s == 7:
                        b = t + 2
                        pe.wait_ge(S["rest1"], at(b, 1))
                        for i in range(TI):
                            last = mm(P_FRONT[:, i * C:i * C + C], hT[:, i * 128:i * 128 + 128], w_vT[:],
                                      start=True, stop=True)
                        last.then_inc(S["v_ready"], 1)
                    if D and 2 <= s < X + 2:
                        b, n = t - 1, s - 2
                        e = (n - 1) % X
                        pe.wait_ge(S["hid_ready"], at(b, X, n))
                        if n == 0:
                            wait(pe, S["f_gated"], b)
                        for i in range(TI):
                            last = mm(P_ACC[:, i * C:i * C + C], hidden[:, n % 2, i * 128:i * 128 + 128],
                                      w_down[:, e, :], start=(n == 0 and i == 0), stop=(n == X - 1),
                                      skip_group_check=True)
                        last.then_inc(S["down_ready"], 1)
                    if Cs and s in (2, 3, 5, 6):
                        probs_v(t, (2, 3, 5, 6).index(s))
                    if Cs and s in (3, 4, 6, 7):
                        y_back(t, (3, 4, 6, 7).index(s))
                    if Bs and s == 8:
                        b = t + 1
                        pe.wait_ge(S["m_part3"], at(b, 1))
                        if A:
                            pe.wait_ge(S["v_saved"], at(b + 1, 1))
                        if D:
                            pe.wait_ge(S["gw_saved"], at(t - 1, 4, 3))
                        tr(P_FRONT[0:96, 0:64].bitcast(BF16), mx_parts[:].rearrange("p i m -> p (i m)"),
                           ident_bf[:]).then_inc(S["mT_ready"], 1)
                    if Cs and s == 10:
                        pe.wait_ge(S["ln2_norm"], at(t, 1))
                        for i in range(TI):
                            last = tr(P_BACK[:, i * 128:i * 128 + 128], xn[1][:, i, :], ident[:])
                        last.then_inc(S["h2x_ready"], 1)
                    if Cs and s == 11:
                        pe.wait_ge(S["h2T_ready"], at(t, 1))
                        for i in range(TI):
                            last = mm(P_BACK[:, i * E:i * E + E], h2T[:, i * 128:i * 128 + 128], router[:],
                                      start=True, stop=True)
                        last.then_inc(S["r_ready"], 1)
                if isinstance(t, int) and t == FIRST:
                    gate_tables()
                if isinstance(t, int) and t == FIRST + 1:
                    pe.wait_ge(S["ga_done"], 4)
                    pe.wait_ge(S["k_mask"], 2)
                    pe.wait_ge(S["ld_ones"], RING * DMA)
                    pe.wait_ge(S["ld_up"], 4 * DMA)
                    pe.wait_ge(S["ld_down"], 2 * DMA)
            pe.wait_ge(S["k_mask"], 2)
            over_slots(pe, slot)


_INS = ['L0_attn_x', 'L0_attn_W_dq', 'L0_attn_W_uq', 'L0_attn_W_dkv', 'L0_attn_W_uk', 'L0_attn_W_uv', 'L0_attn_W_o',
        'L0_ffn_router_w', 'L0_ffn_expert_bias', 'L0_ffn_w1', 'L0_ffn_w2', 'L0_ffn_w3', 'L0_ffn_sw1', 'L0_ffn_sw2',
        'L0_ffn_sw3', 'L0_c', 'L0_wmod']


def kernel(**inputs):
    import numpy as np
    import concourse.bacc as bacc
    from concourse.bass_utils import run_bass_kernel_spmd

    nc = bacc.Bacc("TRN2", target_bir_lowering=False, num_devices=1)
    arrays, args = {}, []
    for name in _INS:
        a = np.ascontiguousarray(inputs[name])
        arrays[f"in_{name}"] = a
        args.append(nc.dram_tensor(f"in_{name}", a.shape, mybir.dt.from_np(a.dtype), kind="ExternalInput").ap())
    out = nc.dram_tensor("out", (B, T, C), F32, kind="ExternalOutput").ap()
    build(nc, *args, out)
    return run_bass_kernel_spmd(nc, [arrays], core_ids=[0]).results[0]["out"]
```

```python
import concourse.bass as bass
import concourse.mybir as mybir
from contextlib import ExitStack

F32 = mybir.dt.float32
BF16 = mybir.dt.bfloat16
ALU = mybir.AluOpType
ACT = mybir.ActivationFunctionType
AX = mybir.AxisListType

B, T, C = 8, 256, 128
NH, HS = 16, 8
E, X = 8, 9
TI = T // 128
PARTS = 3
ROWS = PARTS * PARTS * HS
MROWS = ROWS + PARTS
SPAN = NH * T
RING = 4
UNITS = 12
GROUPS = NH // 4
SCALE = float(HS) ** -0.5
EPS = 1e-5
MASKED = -1.0e38
STEPS = 15
HEADS_IN = (2, 3, 5, 6)
HEADS_OUT = (3, 4, 6, 7)
UP = 3

FIRST, LAST = -3, B
STEADY = range(2, B - 3)
DMA = 16


def at(b, per, k=0):
    return b * per + k + 1


def wait(eng, sem, value):
    if not (isinstance(value, int) and value <= 0):
        eng.wait_ge(sem, value)


def alone(eng):
    eng.nop(nofuse=True)


def cols(b, width, start=0, n=None):
    return bass.ds(b * width + start, width if n is None else n)


def ring(b, start=0, n=SPAN):
    return bass.ds((b % RING) * SPAN + start, n)


def over_slots(eng, slot):
    def stages(t):
        return [0 <= t + d < B for d in (3, 2, 1, 0, -1)]
    for t in range(FIRST, STEADY.start):
        slot(t, *stages(t))
    with eng.Fori(STEADY.start, STEADY.stop) as t:
        slot(t, True, True, True, True, True)
    for t in range(STEADY.stop, LAST + 1):
        slot(t, *stages(t))


def build(nc, x, W_dq, W_uq, W_dkv, W_uk, W_uv, W_o, router_w, expert_bias,
          w1, w2, w3, sw1, sw2, sw3, c, wmod, out):
    ctx = ExitStack()
    with ctx:
        def sb(name, shape, dt=F32):
            return ctx.enter_context(nc.sbuf_tensor(name, shape, dt))

        def sem(name):
            return ctx.enter_context(nc.semaphore(name))

        qk_dram = nc.dram_tensor("qk_parts", (B, 2, PARTS, HS * NH, T), BF16, kind="Internal").ap()

        ident = sb("ident", [128, 128])
        ident_bf = sb("ident_bf", [128, 128], BF16)
        causal = sb("causal", [128, 4, 128], BF16)
        ones_rows = sb("ones_rows", [PARTS, SPAN], BF16)
        neg_half = sb("neg_half", [128, TI])
        earlier = sb("earlier", [128, E, E])
        wdq = sb("wdq", [32, C]); wuq = sb("wuq", [C, 32]); wdkv = sb("wdkv", [32, C])
        wuk = sb("wuk", [C, 32]); wuv = sb("wuv", [C, 32]); wo = sb("wo", [C, C])
        wuqT = sb("wuqT", [32, C]); woT = sb("woT", [C, C])
        w_qT = sb("w_qT", [C, C]); w_q = sb("w_q", [C, C]); v_eff = sb("v_eff", [32, C])
        k_effT = sb("k_effT", [32, C]); w_kT = sb("w_kT", [C, C]); w_vT = sb("w_vT", [C, C])
        c_sb = sb("c_sb", [B, C]); cT = sb("cT", [C, B]); c_tanh = sb("c_tanh", [C, B])
        c_sig = sb("c_sig", [C, B]); c_silu = sb("c_silu", [C, B]); c_wide = sb("c_wide", [C, B, C])
        wm = sb("wm", [C, 6 * C])
        mod = sb("mod", [C, 4, B])
        gate_att = sb("gate_att", [128, B * C])
        gate_ffn = sb("gate_ffn", [128, B * C])
        router = sb("router", [C, E]); bias = sb("bias", [128, E])
        w_up = sb("w_up", [C, X, 2, C]); w_down = sb("w_down", [C, X, C])
        x_sb = sb("x_sb", [128, B * TI * C]); x2_sb = sb("x2_sb", [128, B * TI * C])
        v_sb = sb("v_sb", [128, B * TI * C])
        q_stack = sb("q_stack", [MROWS, RING * SPAN], BF16)
        k_stack = sb("k_stack", [MROWS, RING * SPAN], BF16)
        stats = [sb(f"stats{n}", [128, TI, 6]) for n in (1, 2)]
        mean_var = [sb(f"mean_var{n}", [128, TI, 2]) for n in (1, 2)]
        var_eps = [sb(f"var_eps{n}", [128, TI]) for n in (1, 2)]
        rstd = [sb(f"rstd{n}", [128, TI]) for n in (1, 2)]
        xn = [sb(f"xn{n}", [128, TI, C]) for n in (1, 2)]
        hT = sb("hT", [C, T]); h2T = sb("h2T", [C, T])
        qk_parts = sb("qk_parts_sb", [128, 2, PARTS, T], BF16)
        qk_rest = sb("qk_rest", [128, 2, T])
        mx = sb("mx", [128, NH, TI])
        mx_parts = sb("mx_parts_sb", [128, PARTS, NH * TI], BF16)
        mx_rest = sb("mx_rest", [128, 2, NH * TI])
        mx_rows = sb("mx_rows", [PARTS * NH * TI, 128], BF16)
        probs = sb("probs", [128, 6, 512])
        v_ones = sb("v_ones", [128, TI, NH, 32])
        yT = sb("yT", [128, 2, T])
        y_rec = sb("y_rec", [128, TI, 4]); y = sb("y", [128, TI, NH, HS])
        y_gated = sb("y_gated", [128, TI, C])
        r_max = sb("r_max", [128, TI]); r_in = sb("r_in", [128, TI, E]); r_exp = sb("r_exp", [128, TI, E])
        r_sum = sb("r_sum", [128, TI]); r_rec = sb("r_rec", [128, TI]); score = sb("score", [128, TI, E])
        biased = sb("biased", [128, TI, E]); above = sb("above", [128, TI, E, E])
        ahead = sb("ahead", [128, TI, E, E])
        equal = sb("equal", [128, TI, E, E]); rank = sb("rank", [128, TI, E]); gates = sb("gates", [128, TI, E])
        gates_wide = sb("gates_wide", [128, E, T])
        g_sign, g_neg, g_abs = probs[:, 0, :], probs[:, 1, :], probs[:, 2, :]
        g_tanh = sb("g_tanh", [128, 2, T]); act_g = sb("act_g", [128, 2, T]); hidden = sb("hidden", [128, 2, T])
        f_out = sb("f_out", [128, TI, C]); o_sb = sb("o_sb", [128, TI, C])

        bank = [ctx.enter_context(nc.psum_tensor(f"bank{i}", [128, 512], F32)) for i in range(8)]
        P_MAX, P_EXP, P_UP, P_ACC, P_FRONT, P_BACK = bank[0], bank[1:3], bank[3:5], bank[5], bank[6], bank[7]

        names = """ld_small ld_c ld_x ld_up ld_down ld_ones k_ident k_mask k_rest k_fill
            t_setup e_setup t_gate e_gate m_tanh m_sig m_silu m_wide gs_step ga_done
            ln1_stats ln1_mv ln1_ve ln1_rstd ln1_norm xT_ready hT_ready qk_ready part1 rest1 part2 part3
            v_ready v_saved qk_stored stacked s1_ready s1_max m_part1 m_rest1 m_part2 m_rest2 m_part3
            mT_ready mT_saved m_stacked
            v_placed s2_ready s2_exp s2_masked pv_ready yT_saved ytr_ready y_recip y_norm y_gate x2_ready
            ln2_stats ln2_mv ln2_ve ln2_rstd ln2_norm h2x_ready h2T_ready r_ready r_maxed r_shifted r_exped
            r_summed r_inv r_score r_biased r_ahead r_above r_equal r_tied r_counted r_ranked r_scored gates_ready
            gw_ready gw_saved up_ready tanhed silued gated hid_ready down_ready f_gated o_ready stored"""
        S = {n: sem(n) for n in names.split()}
        block = ctx.enter_context(nc.Block())
        N_SETUP = 4

        @block.sync
        def _(sp):
            for dst, src in ((wuq, W_uq), (wo, W_o), (wdq, W_dq), (wuk, W_uk), (wuv, W_uv), (wdkv, W_dkv)):
                sp.dma_start(dst[:], src).then_inc(S["ld_small"], DMA)
            sp.dma_start(w_up[:, 0:E, 0, :], w1.rearrange("e d h -> d e h")).then_inc(S["ld_up"], DMA)
            sp.dma_start(w_up[:, 0:E, 1, :], w3.rearrange("e d h -> d e h")).then_inc(S["ld_up"], DMA)
            sp.dma_start(w_up[:, E, 0, :], sw1).then_inc(S["ld_up"], DMA)
            sp.dma_start(w_up[:, E, 1, :], sw3).then_inc(S["ld_up"], DMA)
            sp.dma_start(w_down[:, 0:E, :], w2.rearrange("e h d -> h e d")).then_inc(S["ld_down"], DMA)
            sp.dma_start(w_down[:, E, :], sw2).then_inc(S["ld_down"], DMA)
            sp.wait_ge(S["k_fill"], 1)
            for b in range(RING):
                sp.dma_start(k_stack[ROWS:MROWS, b * SPAN:(b + 1) * SPAN], ones_rows[:, :]).then_inc(S["ld_ones"], DMA)

            def slot(t, LN, A, Bs, Cs, D):
                if A:
                    b = t + 2
                    sp.wait_ge(S["part3"], at(b, 1))
                    sp.dma_start(qk_dram[bass.ds(b, 1)].rearrange("b s i r t -> r (b s i) t"),
                                 qk_parts[:].rearrange("r s i t -> r (s i) t")).then_inc(S["qk_stored"], DMA)
                    sp.wait_ge(S["qk_stored"], b * DMA + DMA)
                    wait(sp, S["s2_ready"], (b - RING + 1) * UNITS)
                    for i in range(PARTS):
                        src = qk_dram[bass.ds(b, 1), 0, i].rearrange("b (d h) t -> (b d) (h t)", d=HS)
                        sp.dma_start(q_stack[24 * i:24 * i + 24, ring(b)],
                                     src.unsqueeze(0).to_broadcast([PARTS, HS, SPAN])).then_inc(S["stacked"], DMA)
                    src = qk_dram[bass.ds(b, 1), 1].rearrange("b i (d h) t -> (b i d) (h t)", d=HS)
                    sp.dma_start(k_stack[0:ROWS, ring(b)],
                                 src.unsqueeze(0).to_broadcast([PARTS, PARTS * HS, SPAN])).then_inc(S["stacked"], DMA)
                if D:
                    b = t - 1
                    sp.wait_ge(S["o_ready"], at(b, 1))
                    sp.dma_start(out[bass.ds(b, 1)].rearrange("b (i p) c -> p (b i) c", p=128), o_sb[:, :, :])\
                      .then_inc(S["stored"], DMA)
            over_slots(sp, slot)
            sp.wait_ge(S["stored"], B * DMA)

        @block.gpsimd
        def _(pool):
            g = nc.gpsimd
            g.memset(ident[:], 0.0).then_inc(S["k_ident"], 1)
            g.memset(ident_bf[:], 0.0).then_inc(S["k_ident"], 1)
            pool.wait_ge(S["k_ident"], 2)
            for m in (ident, ident_bf):
                g.affine_select(out=m[:], in_=m[:], compare_op=ALU.not_equal, fill=1.0, base=0,
                                pattern=[[-1, 128]], channel_multiplier=1).then_inc(S["k_ident"], 1)
            g.memset(ones_rows[:], 1.0).then_inc(S["k_fill"], 1)
            g.memset(neg_half[:], -0.5).then_inc(S["k_rest"], 1)
            g.memset(causal[:], 0.0).then_inc(S["k_mask"], 1)
            g.memset(earlier[:], 1.0).then_inc(S["k_rest"], 1)
            g.memset(v_ones[:], 0.0).then_inc(S["k_rest"], 1)
            pool.wait_ge(S["k_mask"], 1)
            g.affine_select(out=causal[:], in_=causal[:], compare_op=ALU.is_ge, fill=MASKED, base=0,
                            pattern=[[0, 4], [-1, 128]], channel_multiplier=1).then_inc(S["k_mask"], 1)
            pool.wait_ge(S["k_rest"], 3)
            g.affine_select(out=earlier[:], in_=earlier[:], compare_op=ALU.is_gt, fill=0.0, base=0,
                            pattern=[[1, E], [-1, E]], channel_multiplier=0).then_inc(S["k_rest"], 1)
            g.memset(v_ones[:, :, :, HS], 1.0).then_inc(S["k_rest"], 1)
            pool.wait_ge(S["k_rest"], 5)

            def inv_std(n, b):
                pool.wait_ge(S[f"ln{n}_mv"], at(b, 1))
                alone(pool)
                g.tensor_scalar(var_eps[n - 1][:], mean_var[n - 1][:, :, 1], EPS, None, ALU.add)\
                 .then_inc(S[f"ln{n}_ve"], 1)
                pool.wait_ge(S[f"ln{n}_ve"], at(b, 1))
                wait(pool, S[f"ln{n}_norm"], b)
                g.tensor_tensor(rstd[n - 1][:], var_eps[n - 1][:], neg_half[:], ALU.pow)\
                 .then_inc(S[f"ln{n}_rstd"], 1)

            def mask(b, u):
                pool.wait_ge(S["s2_exp"], at(b, UNITS, u))
                alone(pool)
                buf = probs[:, u % 6, :]
                v = buf.rearrange("k (h q) -> k h q", h=4) if u % 3 == 2 else \
                    buf.rearrange("k (h q) -> k h q", h=2)[:, :, 0:128]
                g.affine_select(out=v, in_=v, compare_op=ALU.is_ge, fill=0.0, base=0,
                                pattern=[[0, 4 if u % 3 == 2 else 2], [1, 128]], channel_multiplier=-1)\
                 .then_inc(S["s2_masked"], 1)

            def slot(t, LN, A, Bs, Cs, D):
                if Cs:
                    pool.wait_ge(S["v_saved"], at(t, 1))
                    wait(pool, S["pv_ready"], t * GROUPS)
                    alone(pool)
                    g.tensor_copy(v_ones[:, :, :, 0:HS],
                                  v_sb[:, cols(t, TI * C)].rearrange("p (i h d) -> p i h d", i=TI, h=NH))\
                     .then_inc(S["v_placed"], 1)
                for s in range(STEPS):
                    if Cs and s < 6:
                        mask(t, 2 * s)
                    if D and 1 <= s - UP < X:
                        b, n = t - 1, s - UP
                        pool.wait_ge(S["silued"], at(b, X, n))
                        pool.wait_ge(S["gw_saved"], at(b, 4, (n - 1) // 2))
                        g.tensor_tensor(act_g[:, n % 2, :], act_g[:, n % 2, :], gates_wide[:, n - 1, :], ALU.mult)\
                         .then_inc(S["gated"], 1)
                    if Cs and s < 6:
                        mask(t, 2 * s + 1)
                    if LN and s == 10:
                        inv_std(1, t + 3)
                    if A and s == 3:
                        b = t + 2
                        pool.wait_ge(S["part2"], at(b, 1))
                        g.tensor_tensor(qk_parts[:, :, 2, :], qk_rest[:], qk_parts[:, :, 1, :], ALU.subtract)\
                         .then_inc(S["part3"], 1)
                    if Bs and s == 7:
                        b = t + 1
                        m = mx[:].rearrange("p h i -> p (h i)")
                        pool.wait_ge(S["s1_max"], at(b, UNITS, UNITS - 1))
                        wait(pool, S["mT_ready"], b)
                        alone(pool)
                        g.tensor_scalar(mx_parts[:, 0], m, -1.0, None, ALU.mult).then_inc(S["m_part1"], 1)
                        pool.wait_ge(S["m_part1"], at(b, 1))
                        g.tensor_tensor(mx_rest[:, 0], m, mx_parts[:, 0], ALU.add).then_inc(S["m_rest1"], 1)
                        pool.wait_ge(S["m_rest1"], at(b, 1))
                        alone(pool)
                        g.tensor_scalar(mx_parts[:, 1], mx_rest[:, 0], -1.0, None, ALU.mult)\
                         .then_inc(S["m_part2"], 1)
                        pool.wait_ge(S["m_part2"], at(b, 1))
                        g.tensor_tensor(mx_rest[:, 1], mx_rest[:, 0], mx_parts[:, 1], ALU.add)\
                         .then_inc(S["m_rest2"], 1)
                        pool.wait_ge(S["m_rest2"], at(b, 1))
                        alone(pool)
                        g.tensor_scalar(mx_parts[:, 2], mx_rest[:, 1], -1.0, None, ALU.mult)\
                         .then_inc(S["m_part3"], 1)
                    if Cs and s == 8:
                        inv_std(2, t)

            pool.wait_ge(S["ld_c"], 4 * DMA)
            over_slots(pool, slot)

        @block.scalar
        def _(act):
            a = nc.scalar
            act.dma_start(c_sb[:], c).then_inc(S["ld_c"], DMA)
            act.dma_start(wm[:], wmod).then_inc(S["ld_c"], DMA)
            for n in range(4):
                k = B * TI // 4
                act.dma_start(x_sb[:, n * k * C:(n + 1) * k * C].rearrange("p (i c) -> p i c", c=C),
                              x.rearrange("b (i p) c -> p (b i) c", p=128)[:, n * k:(n + 1) * k, :])\
                   .then_inc(S["ld_x"], DMA)
            act.dma_start(router[:], router_w).then_inc(S["ld_c"], DMA)
            act.dma_start(bias[:], expert_bias.unsqueeze(0).to_broadcast([128, E])).then_inc(S["ld_c"], DMA)
            act.wait_ge(S["e_setup"], 1)
            a.activation(c_tanh[:], cT[:], ACT.Tanh, scale=0.5).then_inc(S["m_tanh"], 1)

            def exps(b, u):
                act.wait_ge(S["s2_ready"], at(b, UNITS, u))
                wait(act, S["pv_ready"], at(b, GROUPS, (u - 6) // 3))
                a.activation(probs[:, u % 6, :], P_EXP[u % 2][:], ACT.Exp, scale=SCALE).then_inc(S["s2_exp"], 1)

            def slot(t, LN, A, Bs, Cs, D):
                for s in range(STEPS):
                    if Cs and s < 6:
                        exps(t, 2 * s)
                    if D and s == 0:
                        b = t - 1
                        act.wait_ge(S["h2x_ready"], at(b, 1))
                        wait(act, S["up_ready"], b * X)
                        a.activation(h2T[:], P_BACK[:, 0:T], ACT.Identity, bias=mod[:, 2, bass.ds(b, 1)],
                                     scale=mod[:, 3, bass.ds(b, 1)]).then_inc(S["h2T_ready"], 1)
                    if D and s == 1:
                        b = t - 1
                        act.wait_ge(S["r_shifted"], at(b, 1))
                        wait(act, S["r_scored"], b)
                        a.activation(r_exp[:], r_in[:], ACT.Exp).then_inc(S["r_exped"], 1)
                    if D and 0 <= s - UP < X:
                        b, n = t - 1, s - UP
                        act.wait_ge(S["up_ready"], at(b, X, n))
                        wait(act, S["silued"], at(b, X, n - 2))
                        a.activation(g_tanh[:, n % 2, :], P_UP[n % 2][:, 0:T], ACT.Tanh, scale=0.5)\
                         .then_inc(S["tanhed"], 1)
                    if D and 4 <= s < 8:
                        b, p = t - 1, s - 4
                        act.wait_ge(S["gw_ready"], at(b, 4, p))
                        wait(act, S["gated"], b * E)
                        a.activation(gates_wide[:, 2 * p:2 * p + 2, :],
                                     P_FRONT[:].rearrange("p (e t) -> p e t", e=2), ACT.Copy)\
                         .then_inc(S["gw_saved"], 1)
                    if Cs and s < 6:
                        exps(t, 2 * s + 1)
                    if Cs and s in HEADS_IN:
                        g = HEADS_IN.index(s)
                        act.wait_ge(S["pv_ready"], at(t, GROUPS, g))
                        wait(act, S["ytr_ready"], at(t, GROUPS, g - 2))
                        a.activation(yT[:, g % 2, :], P_BACK[:, 0:T], ACT.Copy).then_inc(S["yT_saved"], 1)
                    if A and s == 1:
                        b = t + 2
                        act.wait_ge(S["xT_ready"], at(b, 1))
                        wait(act, S["v_ready"], b)
                        a.activation(hT[:], P_FRONT[:, 0:T], ACT.Identity, bias=mod[:, 0, bass.ds(b, 1)],
                                     scale=mod[:, 1, bass.ds(b, 1)]).then_inc(S["hT_ready"], 1)
                    if A and s == 2:
                        b = t + 2
                        act.wait_ge(S["qk_ready"], at(b, 1))
                        wait(act, S["qk_stored"], b * DMA)
                        a.activation(qk_parts[:, :, 0, :], P_FRONT[:].rearrange("p (s t) -> p s t", s=2), ACT.Copy)\
                         .then_inc(S["part1"], 1)
                    if A and s == 3:
                        b = t + 2
                        act.wait_ge(S["rest1"], at(b, 1))
                        a.activation(qk_parts[:, :, 1, :], qk_rest[:], ACT.Copy).then_inc(S["part2"], 1)
                    if Bs and s == 8:
                        b = t + 1
                        act.wait_ge(S["mT_ready"], at(b, 1))
                        wait(act, S["m_stacked"], b * DMA)
                        a.activation(mx_rows[:], P_FRONT[0:96, 0:64].bitcast(BF16), ACT.Copy)\
                         .then_inc(S["mT_saved"], 1)
                        act.wait_ge(S["mT_saved"], at(b, 1))
                        act.dma_start(q_stack[ROWS:MROWS, ring(b)], mx_rows[:, :]).then_inc(S["m_stacked"], DMA)
            act.wait_ge(S["e_setup"], N_SETUP + 1)
            over_slots(act, slot)

        @block.vector
        def _(dve):
            v = nc.vector
            dve.wait_ge(S["t_setup"], 1)
            v.tensor_copy(cT[:], bank[0][:, 0:B])
            v.tensor_copy(wuqT[:], bank[0][0:32, 128:256])
            v.tensor_copy(woT[:], bank[0][:, 256:384]).then_inc(S["e_setup"], 1)
            dve.wait_ge(S["t_setup"], 2)
            v.tensor_copy(w_qT[:].rearrange("c (d h) -> c d h", d=HS),
                          bank[1][:, 0:128].rearrange("c (h d) -> c d h", h=NH))
            v.tensor_copy(w_q[:], bank[1][:, 128:256])
            v.tensor_copy(v_eff[:], bank[1][0:32, 256:384]).then_inc(S["e_setup"], 1)
            dve.wait_ge(S["t_setup"], 3)
            v.tensor_copy(k_effT[:], bank[2][0:32, 0:128]).then_inc(S["e_setup"], 1)
            dve.wait_ge(S["m_tanh"], 1)
            v.tensor_scalar(c_sig[:], c_tanh[:], 1.0, 0.5, ALU.add, ALU.mult).then_inc(S["m_sig"], 1)
            dve.wait_ge(S["m_sig"], 1)
            v.tensor_tensor(c_silu[:], c_sig[:], cT[:], ALU.mult).then_inc(S["m_silu"], 1)
            dve.wait_ge(S["t_setup"], 4)
            v.tensor_copy(w_kT[:].rearrange("c (d h) -> c d h", d=HS),
                          bank[3][:, 0:128].rearrange("c (h d) -> c d h", h=NH))
            v.tensor_copy(w_vT[:], bank[3][:, 128:256]).then_inc(S["e_setup"], 1)
            dve.wait_ge(S["m_silu"], 1)
            v.tensor_copy(c_wide[:], c_silu[:].unsqueeze(2).to_broadcast([C, B, C])).then_inc(S["m_wide"], 1)
            dve.wait_ge(S["t_setup"], 5)
            for n, plus in enumerate((0.0, 1.0, 0.0, 1.0)):
                last = v.tensor_scalar(mod[:, n], bank[4][:, n * B:n * B + B], plus, None, ALU.add)
            last.then_inc(S["e_setup"], 1)

            def gate_tables():
                for n in range(4):
                    half = n % 2
                    dst = (gate_att if n < 2 else gate_ffn)[:, half * 512:half * 512 + 512]
                    f = 1.0 if n < 2 else 0.5
                    dve.wait_ge(S["t_gate"], n + 1)
                    wait(dve, S["ga_done"], n)
                    v.tensor_scalar(g_sign, bank[(3, 4, 5, 7)[n]][:], 0.0, 2.0 * f, ALU.is_ge, ALU.mult)
                    v.tensor_scalar(g_neg, bank[(3, 4, 5, 7)[n]][:], -1.0, None, ALU.mult)\
                     .then_inc(S["gs_step"], 1)
                    dve.wait_ge(S["gs_step"], 2 * n + 1)
                    v.scalar_tensor_tensor(g_abs, g_neg, 0.25, bank[(3, 4, 5, 7)[n]][:], ALU.max, ALU.max)\
                     .then_inc(S["gs_step"], 1)
                    dve.wait_ge(S["gs_step"], 2 * n + 2)
                    v.scalar_tensor_tensor(dst, g_sign, -f, g_abs, ALU.add, ALU.mult)\
                     .then_inc(S["ga_done"], 1)

            def ln_stats(n, b, src):
                wait(dve, S[f"ln{n}_norm"], b)
                alone(dve)
                for i in range(TI):
                    last = v.bn_stats(stats[n - 1][:, i], src[:, cols(b, TI * C, i * C, C)])
                last.then_inc(S[f"ln{n}_stats"], 1)
                dve.wait_ge(S[f"ln{n}_stats"], at(b, 1))
                alone(dve)
                for i in range(TI):
                    last = v.bn_aggr(mean_var[n - 1][:, i], stats[n - 1][:, i])
                last.then_inc(S[f"ln{n}_mv"], 1)

            def ln_norm(n, b, src, used):
                dve.wait_ge(S[f"ln{n}_rstd"], at(b, 1))
                wait(dve, S[used], b)
                for i in range(TI):
                    last = v.tensor_scalar(xn[n - 1][:, i], src[:, cols(b, TI * C, i * C, C)],
                                           mean_var[n - 1][:, i, 0:1], rstd[n - 1][:, i:i + 1],
                                           ALU.subtract, ALU.mult)
                last.then_inc(S[f"ln{n}_norm"], 1)

            def row_max(b, u):
                dve.wait_ge(S["s1_ready"], at(b, UNITS, u))
                if u == 0:
                    wait(dve, S["m_part3"], b)
                if u < 4:
                    dst, n = mx[:, 4 * u:4 * u + 4, 0], 4
                else:
                    dst, n = mx[:, 2 * (u - 4):2 * (u - 4) + 2, 1], 2
                v.tensor_reduce(dst, P_MAX[:].rearrange("p (h k) -> p h k", h=n), AX.X, ALU.max)\
                 .then_inc(S["s1_max"], 1)

            def hidden_of(b, n):
                if n == 0:
                    dve.wait_ge(S["silued"], at(b, X, 0))
                else:
                    dve.wait_ge(S["gated"], at(b, E, n - 1))
                wait(dve, S["down_ready"], at(b, X, n - 2))
                v.tensor_tensor(hidden[:, n % 2, :], P_UP[n % 2][:, T:2 * T], act_g[:, n % 2, :], ALU.mult)\
                 .then_inc(S["hid_ready"], 1)

            def step(sem_name, b, instruction):
                instruction.then_inc(S[sem_name], 1)
                dve.wait_ge(S[sem_name], at(b, 1))

            def route(b):
                src = P_BACK[:, 0:TI * E].rearrange("p (i e) -> p i e", i=TI)
                dve.wait_ge(S["r_ready"], at(b, 1))
                step("r_maxed", b, v.tensor_reduce(r_max[:], src, AX.X, ALU.max))
                v.tensor_tensor(r_in[:], src, r_max[:].unsqueeze(2).to_broadcast([128, TI, E]),
                                ALU.subtract).then_inc(S["r_shifted"], 1)
                dve.wait_ge(S["r_exped"], at(b, 1))
                step("r_summed", b, v.tensor_reduce(r_sum[:], r_exp[:], AX.X, ALU.add))
                step("r_inv", b, v.reciprocal(r_rec[:], r_sum[:]))
                step("r_scored", b, v.tensor_tensor(score[:], r_exp[:],
                                                    r_rec[:].unsqueeze(2).to_broadcast([128, TI, E]), ALU.mult))
                step("r_biased", b, v.tensor_tensor(biased[:], score[:],
                                                    bias[:].unsqueeze(1).to_broadcast([128, TI, E]), ALU.add))
                other = biased[:].unsqueeze(2).to_broadcast([128, TI, E, E])
                own = biased[:].unsqueeze(3).to_broadcast([128, TI, E, E])
                v.tensor_tensor(above[:], other, own, ALU.is_gt).then_inc(S["r_above"], 1)
                step("r_equal", b, v.tensor_tensor(equal[:], other, own, ALU.is_equal))
                step("r_tied", b, v.tensor_tensor(equal[:], equal[:],
                                                  earlier[:].unsqueeze(1).to_broadcast([128, TI, E, E]), ALU.mult))
                step("r_counted", b, v.tensor_tensor(above[:], above[:], equal[:], ALU.add))
                step("r_ranked", b, v.tensor_reduce(rank[:], above[:], AX.X, ALU.add))
                wait(dve, S["gw_ready"], b * 4)
                v.scalar_tensor_tensor(gates[:], rank[:], 1.5, score[:], ALU.is_lt, ALU.mult)\
                 .then_inc(S["gates_ready"], 1)

            def slot(t, LN, A, Bs, Cs, D):
                for s in range(STEPS):
                    if Bs and s < 6:
                        row_max(t + 1, 2 * s)
                    if D and 0 <= s - UP < X:
                        b, n = t - 1, s - UP
                        dve.wait_ge(S["tanhed"], at(b, X, n))
                        wait(dve, S["hid_ready"], at(b, X, n - 2))
                        v.scalar_tensor_tensor(act_g[:, n % 2, :], g_tanh[:, n % 2, :], 1.0,
                                               P_UP[n % 2][:, 0:T], ALU.add, ALU.mult)\
                         .then_inc(S["silued"], 1)
                    if Bs and s < 6:
                        row_max(t + 1, 2 * s + 1)
                    if D and s == 1:
                        route(t - 1)
                    if D and 1 <= s - UP <= X:
                        hidden_of(t - 1, s - UP - 1)
                    if LN and s == 10:
                        b = t + 3
                        dve.wait_ge(S["ld_x"], 4 * DMA)
                        ln_stats(1, b, x_sb)
                    if LN and s == 11:
                        ln_norm(1, t + 3, x_sb, "xT_ready")
                    if Cs and s in HEADS_OUT:
                        g = HEADS_OUT.index(s)
                        src = P_BACK[:, 0:T].rearrange("p (i h r) -> p i h r", i=TI, h=4)
                        dve.wait_ge(S["ytr_ready"], at(t, GROUPS, g))
                        wait(dve, S["y_norm"], at(t, GROUPS, g - 1))
                        v.reciprocal(y_rec[:], src[:, :, :, HS]).then_inc(S["y_recip"], 1)
                        dve.wait_ge(S["y_recip"], at(t, GROUPS, g))
                        if g == 0:
                            wait(dve, S["y_gate"], t)
                        v.tensor_tensor(y[:, :, 4 * g:4 * g + 4, :], src[:, :, :, 0:HS],
                                        y_rec[:].unsqueeze(3).to_broadcast([128, TI, 4, HS]), ALU.mult)\
                         .then_inc(S["y_norm"], 1)
                    if A and s == 2:
                        b = t + 2
                        dve.wait_ge(S["part1"], at(b, 1))
                        wait(dve, S["part3"], b)
                        v.tensor_tensor(qk_rest[:], P_FRONT[:].rearrange("p (s t) -> p s t", s=2),
                                        qk_parts[:, :, 0, :], ALU.subtract).then_inc(S["rest1"], 1)
                    if A and s == 3:
                        b = t + 2
                        dve.wait_ge(S["v_ready"], at(b, 1))
                        v.tensor_copy(v_sb[:, cols(b, TI * C)], P_FRONT[:, 0:TI * C]).then_inc(S["v_saved"], 1)
                    if Cs and s == 8:
                        dve.wait_ge(S["y_norm"], at(t, GROUPS, GROUPS - 1))
                        wait(dve, S["x2_ready"], t)
                        v.tensor_tensor(y_gated[:], y[:].rearrange("p i h d -> p i (h d)"),
                                        gate_att[:, cols(t, C)].unsqueeze(1).to_broadcast([128, TI, C]),
                                        ALU.mult).then_inc(S["y_gate"], 1)
                        dve.wait_ge(S["y_gate"], at(t, 1))
                        v.tensor_tensor(x2_sb[:, cols(t, TI * C)], x_sb[:, cols(t, TI * C)],
                                        y_gated[:].rearrange("p i c -> p (i c)"), ALU.add)\
                         .then_inc(S["x2_ready"], 1)
                        dve.wait_ge(S["x2_ready"], at(t, 1))
                        ln_stats(2, t, x2_sb)
                    if Cs and s == 9:
                        ln_norm(2, t, x2_sb, "h2x_ready")
                    if D and s == STEPS - 1:
                        b = t - 1
                        dve.wait_ge(S["down_ready"], at(b, X, X - 1))
                        wait(dve, S["o_ready"], b)
                        v.tensor_tensor(f_out[:], P_ACC[:, 0:TI * C].rearrange("p (i c) -> p i c", i=TI),
                                        gate_ffn[:, cols(b, C)].unsqueeze(1).to_broadcast([128, TI, C]),
                                        ALU.mult).then_inc(S["f_gated"], 1)
                        dve.wait_ge(S["f_gated"], at(b, 1))
                        wait(dve, S["stored"], b * DMA)
                        v.tensor_tensor(o_sb[:].rearrange("p i c -> p (i c)"), f_out[:].rearrange("p i c -> p (i c)"),
                                        x2_sb[:, cols(b, TI * C)], ALU.add).then_inc(S["o_ready"], 1)
                if isinstance(t, int) and t == FIRST + 1:
                    gate_tables()
            over_slots(dve, slot)

        @block.tensor
        def _(pe):
            mm, tr = nc.tensor.matmul, nc.tensor.transpose
            pe.wait_ge(S["k_ident"], 4)
            pe.wait_ge(S["ld_small"], 6 * DMA)
            pe.wait_ge(S["ld_c"], 4 * DMA)
            tr(bank[0][:, 0:B], c_sb[:], ident[0:B, 0:B])
            tr(bank[0][0:32, 128:256], wuq[:], ident[:])
            tr(bank[0][:, 256:384], wo[:], ident[:]).then_inc(S["t_setup"], 1)
            pe.wait_ge(S["e_setup"], 1)
            mm(bank[1][:, 0:128], wdq[:], wuqT[:], start=True, stop=True)
            mm(bank[1][:, 128:256], wuqT[:], wdq[:], start=True, stop=True)
            mm(bank[1][0:32, 256:384], wuv[:], woT[:], start=True, stop=True).then_inc(S["t_setup"], 1)
            pe.wait_ge(S["e_setup"], 2)
            mm(bank[2][0:32, 0:128], wuk[:], w_q[:], start=True, stop=True).then_inc(S["t_setup"], 1)
            pe.wait_ge(S["e_setup"], 3)
            mm(bank[3][:, 0:128], wdkv[:], k_effT[:], start=True, stop=True)
            mm(bank[3][:, 128:256], wdkv[:], v_eff[:], start=True, stop=True).then_inc(S["t_setup"], 1)
            pe.wait_ge(S["m_silu"], 1)
            for n, s in enumerate((0, 1, 3, 4)):
                last = mm(bank[4][:, n * B:n * B + B], wm[:, s * C:(s + 1) * C], c_silu[:], start=True, stop=True)
            last.then_inc(S["t_setup"], 1)
            pe.wait_ge(S["e_setup"], N_SETUP + 1)

            def gate_tables():
                pe.wait_ge(S["m_wide"], 1)
                for n in range(4):
                    s = 2 if n < 2 else 5
                    for k in range(4):
                        last = mm(bank[(3, 4, 5, 7)[n]][:, k * C:(k + 1) * C], c_wide[:, 4 * (n % 2) + k, :],
                                  wm[:, s * C:(s + 1) * C], start=True, stop=True)
                    last.then_inc(S["t_gate"], 1)

            def max_unit(b, u):
                wait(pe, S["s1_max"], b * UNITS + u)
                if u == 0:
                    pe.wait_ge(S["stacked"], b * 4 * DMA + 4 * DMA)
                if u < 4:
                    mm(P_MAX[:], ident_bf[:], causal[:].rearrange("p h k -> p (h k)"), start=True, stop=False,
                       skip_group_check=True)
                    for j in range(4):
                        h = 4 * u + j
                        last = mm(P_MAX[:, j * 128:j * 128 + 128], q_stack[0:ROWS, ring(b, h * T, 128)],
                                  k_stack[0:ROWS, ring(b, h * T, 128)], start=False, stop=(j == 3),
                                  skip_group_check=True)
                else:
                    mm(P_MAX[:].rearrange("p (h k) -> p h k", h=2)[:, :, 128:256], ident_bf[:], causal[:, 0:2, :],
                       start=True, stop=False, skip_group_check=True)
                    for j in range(2):
                        h = 2 * (u - 4) + j
                        last = mm(P_MAX[:, j * T:j * T + T], q_stack[0:ROWS, ring(b, h * T + 128, 128)],
                                  k_stack[0:ROWS, ring(b, h * T, T)], start=False, stop=(j == 1),
                                  skip_group_check=True)
                last.then_inc(S["s1_ready"], 1)

            def exp_unit(b, u):
                wait(pe, S["s2_exp"], b * UNITS + u - 1)
                if u == 0:
                    pe.wait_ge(S["m_stacked"], b * DMA + DMA)
                g, r = divmod(u, 3)
                if r < 2:
                    for j in range(2):
                        h = 4 * g + 2 * r + j
                        last = mm(P_EXP[u % 2][:, j * T:j * T + T], k_stack[:, ring(b, h * T, 128)],
                                  q_stack[:, ring(b, h * T, T)], start=True, stop=True)
                else:
                    for j in range(4):
                        h = 4 * g + j
                        last = mm(P_EXP[u % 2][:, j * 128:j * 128 + 128],
                                  k_stack[:, ring(b, h * T + 128, 128)],
                                  q_stack[:, ring(b, h * T + 128, 128)], start=True, stop=True)
                last.then_inc(S["s2_ready"], 1)

            def probs_v(b, g):
                pe.wait_ge(S["s2_masked"], at(b, UNITS, 3 * g + 2))
                if g == 0:
                    pe.wait_ge(S["v_placed"], at(b, 1))
                    wait(pe, S["r_shifted"], b)
                elif g == 2:
                    pe.wait_ge(S["y_norm"], at(b, GROUPS, 1))
                else:
                    pe.wait_ge(S["yT_saved"], at(b, GROUPS, g - 1))
                for j in range(4):
                    unit = probs[:, (3 * g + 2) % 6, :]
                    mm(P_BACK[32 * j:32 * j + 32, 128:T], v_ones[:, 1, 4 * g + j, :],
                       unit[:, j * 128:j * 128 + 128], start=True, stop=False, skip_group_check=True)
                for j in range(4):
                    unit = probs[:, (3 * g + j // 2) % 6, :]
                    last = mm(P_BACK[32 * j:32 * j + 32, 0:T], v_ones[:, 0, 4 * g + j, :],
                              unit[:, (j % 2) * T:(j % 2) * T + T], start=False, stop=True,
                              skip_group_check=True)
                last.then_inc(S["pv_ready"], 1)

            def y_back(b, g):
                pe.wait_ge(S["yT_saved"], at(b, GROUPS, g | 1))
                if g % 2:
                    pe.wait_ge(S["y_norm"], at(b, GROUPS, g - 1))
                for i in range(TI):
                    last = tr(P_BACK[:, i * 128:i * 128 + 128], yT[:, g % 2, i * 128:i * 128 + 128], ident[:])
                last.then_inc(S["ytr_ready"], 1)

            def slot(t, LN, A, Bs, Cs, D):
                for s in range(STEPS):
                    if Cs and s < 6:
                        exp_unit(t, 2 * s)
                    if Bs and s < 6:
                        max_unit(t + 1, 2 * s)
                    if D and s == 0:
                        b = t - 1
                        pe.wait_ge(S["ln2_norm"], at(b, 1))
                        for i in range(TI):
                            last = tr(P_BACK[:, i * 128:i * 128 + 128], xn[1][:, i, :], ident[:])
                        last.then_inc(S["h2x_ready"], 1)
                    if D and s == 1:
                        b = t - 1
                        pe.wait_ge(S["h2T_ready"], at(b, 1))
                        for i in range(TI):
                            last = mm(P_BACK[:, i * E:i * E + E], h2T[:, i * 128:i * 128 + 128], router[:],
                                      start=True, stop=True)
                        last.then_inc(S["r_ready"], 1)
                    if D and 0 <= s - UP < X:
                        b, n = t - 1, s - UP
                        e = (n - 1) % X
                        wait(pe, S["hid_ready"], at(b, X, n - 2))
                        for k in range(2):
                            last = mm(P_UP[n % 2][:, k * T:k * T + T], w_up[:, e, k, :], h2T[:],
                                      start=True, stop=True)
                        last.then_inc(S["up_ready"], 1)
                    if Cs and s < 6:
                        exp_unit(t, 2 * s + 1)
                    if Bs and s < 6:
                        max_unit(t + 1, 2 * s + 1)
                    if D and 4 <= s < 8:
                        b, p = t - 1, s - 4
                        if p == 0:
                            pe.wait_ge(S["gates_ready"], at(b, 1))
                            if A:
                                pe.wait_ge(S["v_saved"], at(t + 2, 1))
                            else:
                                pe.wait_ge(S["mT_saved"], min(t + 1, B))
                        wait(pe, S["gw_saved"], at(b, 4, p - 1))
                        for k in range(2):
                            for i in range(TI):
                                last = tr(P_FRONT[:, k * T + i * 128:k * T + i * 128 + 128],
                                          gates[:, i, 2 * p + k:2 * p + k + 1].to_broadcast([128, 128]),
                                          ident[:])
                        last.then_inc(S["gw_ready"], 1)
                    if A and s == 1:
                        b = t + 2
                        pe.wait_ge(S["ln1_norm"], at(b, 1))
                        wait(pe, S["v_saved"], b)
                        wait(pe, S["mT_saved"], b - 1)
                        for i in range(TI):
                            last = tr(P_FRONT[:, i * 128:i * 128 + 128], xn[0][:, i, :], ident[:])
                        last.then_inc(S["xT_ready"], 1)
                    if A and s == 2:
                        b = t + 2
                        pe.wait_ge(S["hT_ready"], at(b, 1))
                        mm(P_FRONT[:, 0:T], w_qT[:], hT[:], start=True, stop=True)
                        mm(P_FRONT[:, T:2 * T], w_kT[:], hT[:], start=True, stop=True).then_inc(S["qk_ready"], 1)
                    if A and s == 3:
                        b = t + 2
                        pe.wait_ge(S["rest1"], at(b, 1))
                        for i in range(TI):
                            last = mm(P_FRONT[:, i * C:i * C + C], hT[:, i * 128:i * 128 + 128], w_vT[:],
                                      start=True, stop=True)
                        last.then_inc(S["v_ready"], 1)
                    if D and 0 <= s - UP - 2 < X:
                        b, n = t - 1, s - UP - 2
                        e = (n - 1) % X
                        pe.wait_ge(S["hid_ready"], at(b, X, n))
                        if n == 0:
                            wait(pe, S["f_gated"], b)
                        for i in range(TI):
                            last = mm(P_ACC[:, i * C:i * C + C], hidden[:, n % 2, i * 128:i * 128 + 128],
                                      w_down[:, e, :], start=(n == 0 and i == 0), stop=(n == X - 1),
                                      skip_group_check=True)
                        last.then_inc(S["down_ready"], 1)
                    if Cs and s in HEADS_IN:
                        probs_v(t, HEADS_IN.index(s))
                    if Cs and s in HEADS_OUT:
                        y_back(t, HEADS_OUT.index(s))
                    if Bs and s == 8:
                        b = t + 1
                        pe.wait_ge(S["m_part3"], at(b, 1))
                        if A:
                            pe.wait_ge(S["v_saved"], at(b + 1, 1))
                        if D:
                            pe.wait_ge(S["gw_saved"], at(t - 1, 4, 3))
                        tr(P_FRONT[0:96, 0:64].bitcast(BF16), mx_parts[:].rearrange("p i m -> p (i m)"),
                           ident_bf[:]).then_inc(S["mT_ready"], 1)
                if isinstance(t, int) and t == FIRST + 1:
                    gate_tables()
                if isinstance(t, int) and t == FIRST + 2:
                    pe.wait_ge(S["ga_done"], 4)
                    pe.wait_ge(S["k_mask"], 2)
                    pe.wait_ge(S["ld_ones"], RING * DMA)
                    pe.wait_ge(S["ld_up"], 4 * DMA)
                    pe.wait_ge(S["ld_down"], 2 * DMA)
            pe.wait_ge(S["k_mask"], 2)
            over_slots(pe, slot)


_INS = ['L0_attn_x', 'L0_attn_W_dq', 'L0_attn_W_uq', 'L0_attn_W_dkv', 'L0_attn_W_uk', 'L0_attn_W_uv', 'L0_attn_W_o',
        'L0_ffn_router_w', 'L0_ffn_expert_bias', 'L0_ffn_w1', 'L0_ffn_w2', 'L0_ffn_w3', 'L0_ffn_sw1', 'L0_ffn_sw2',
        'L0_ffn_sw3', 'L0_c', 'L0_wmod']


def kernel(**inputs):
    import numpy as np
    import concourse.bacc as bacc
    from concourse.bass_utils import run_bass_kernel_spmd

    nc = bacc.Bacc("TRN2", target_bir_lowering=False, num_devices=1)
    arrays, args = {}, []
    for name in _INS:
        a = np.ascontiguousarray(inputs[name])
        arrays[f"in_{name}"] = a
        args.append(nc.dram_tensor(f"in_{name}", a.shape, mybir.dt.from_np(a.dtype), kind="ExternalInput").ap())
    out = nc.dram_tensor("out", (B, T, C), F32, kind="ExternalOutput").ap()
    build(nc, *args, out)
    return run_bass_kernel_spmd(nc, [arrays], core_ids=[0]).results[0]["out"]
```

```python
import concourse.bass as bass
import concourse.mybir as mybir
from contextlib import ExitStack

F32 = mybir.dt.float32
BF16 = mybir.dt.bfloat16
ALU = mybir.AluOpType
ACT = mybir.ActivationFunctionType
AX = mybir.AxisListType

B, T, C = 8, 256, 128
NH, HS = 16, 8
E, X = 8, 9
TI = T // 128
PARTS = 3
ROWS = PARTS * PARTS * HS
MROWS = ROWS + PARTS
SPAN = NH * T
RING = 4
UNITS = 12
GROUPS = NH // 4
SCALE = float(HS) ** -0.5
EPS = 1e-5
MASKED = -1.0e38
STEPS = 12

LN1, LN1_NORM, X_T, QK, V = 0, 1, 2, 3, 4
MAX = 10
M_SPLIT, M_T = 22, 24
EXP = 28
PV, Y_T = EXP + 4, EXP + 5
RES = Y_T + 10
LN2, LN2_NORM, H_T, ROUTE = RES + 1, RES + 2, RES + 4, RES + 5
SOFTMAX, COMPARE, GATES = ROUTE + 1, ROUTE + 2, ROUTE + 3
UP = ROUTE + 1
HID, DOWN, ADD = UP + 1, UP + 2, UP + 3
OUT = ADD + X

EARLY = 4
AHEAD = range(2, 4)

SLOTS = B + OUT // STEPS
STEADY = range(OUT // STEPS + 1, B)
DMA = 16


def at(b, per, k=0):
    return b * per + k + 1


def wait(eng, sem, value):
    if not (isinstance(value, int) and value <= 0):
        eng.wait_ge(sem, value)


def alone(eng):
    eng.nop(nofuse=True)


def cols(b, width, start=0, n=None):
    return bass.ds(b * width + start, width if n is None else n)


def ring(b, start=0, n=SPAN):
    return bass.ds((b % RING) * SPAN + start, n)


def over_slots(eng, slot):
    for t in range(0, STEADY.start):
        slot(t)
    with eng.Fori(STEADY.start, STEADY.stop) as t:
        slot(t)
    for t in range(STEADY.stop, SLOTS):
        slot(t)


def when(step, b):
    if step <= V and b == 1:
        return step + EARLY
    if step <= V and b in AHEAD:
        b -= 1
    return b * STEPS + step


def due(t, s, first, count=1, every=1):
    for k in range(count):
        step = first + k * every
        if isinstance(t, int):
            for b in range(B):
                if when(step, b) == t * STEPS + s:
                    yield b, k
        elif step % STEPS == s:
            yield t - step // STEPS, k


def wait_turn(pe, turns, me, b):
    def place(name, entry):
        step = turns[name][0]
        return (when(step, entry) if isinstance(b, int) else entry * STEPS + step), list(turns).index(name)

    entries = range(B) if isinstance(b, int) else range(-len(turns), 1)
    mine = b if isinstance(b, int) else 0
    before = [(place(name, entry), name, entry) for name in turns for entry in entries
              if place(name, entry) < place(me, mine)]
    if before:
        _, name, entry = max(before)
        _, sem, per, k = turns[name]
        pe.wait_ge(sem, at(entry if isinstance(b, int) else b + entry, per, k))


def build(nc, x, W_dq, W_uq, W_dkv, W_uk, W_uv, W_o, router_w, expert_bias,
          w1, w2, w3, sw1, sw2, sw3, c, wmod, out):
    ctx = ExitStack()
    with ctx:
        def sb(name, shape, dt=F32):
            return ctx.enter_context(nc.sbuf_tensor(name, shape, dt))

        def sem(name):
            return ctx.enter_context(nc.semaphore(name))

        qk_dram = nc.dram_tensor("qk_parts", (B, 2, PARTS, HS * NH, T), BF16, kind="Internal").ap()

        ident = sb("ident", [128, 128])
        ident_bf = sb("ident_bf", [128, 128], BF16)
        causal = sb("causal", [128, 4, 128], BF16)
        ones_rows = sb("ones_rows", [PARTS, SPAN], BF16)
        neg_half = sb("neg_half", [128, TI])
        earlier = sb("earlier", [128, E, E])
        wdq = sb("wdq", [32, C]); wuq = sb("wuq", [C, 32]); wdkv = sb("wdkv", [32, C])
        wuk = sb("wuk", [C, 32]); wuv = sb("wuv", [C, 32]); wo = sb("wo", [C, C])
        wuqT = sb("wuqT", [32, C]); woT = sb("woT", [C, C])
        w_qT = sb("w_qT", [C, C]); w_q = sb("w_q", [C, C]); v_eff = sb("v_eff", [32, C])
        k_effT = sb("k_effT", [32, C]); w_kT = sb("w_kT", [C, C]); w_vT = sb("w_vT", [C, C])
        c_sb = sb("c_sb", [B, C]); cT = sb("cT", [C, B]); c_tanh = sb("c_tanh", [C, B])
        c_sig = sb("c_sig", [C, B]); c_silu = sb("c_silu", [C, B])
        entry_row = sb("entry_row", [B, B, 128])
        g_sign = sb("g_sign", [B, 2 * C]); g_neg = sb("g_neg", [B, 2 * C]); g_abs = sb("g_abs", [B, 2 * C])
        g_rows = sb("g_rows", [B, 2 * C])
        wm = sb("wm", [C, 6 * C])
        mod = sb("mod", [C, 4, B])
        res_gates = sb("res_gates", [128, B * 2 * C])
        router = sb("router", [C, E]); bias = sb("bias", [128, E])
        w_up = sb("w_up", [C, X, 2, C]); w_down = sb("w_down", [C, X, C])
        x_sb = sb("x_sb", [128, B * TI * C]); x2_sb = sb("x2_sb", [128, B * TI * C])
        v_sb = sb("v_sb", [128, B * TI * C])
        q_stack = sb("q_stack", [MROWS, RING * SPAN], BF16)
        k_stack = sb("k_stack", [MROWS, RING * SPAN], BF16)
        stats = [sb(f"stats{n}", [128, TI, 6]) for n in (1, 2)]
        mean_var = [sb(f"mean_var{n}", [128, TI, 2]) for n in (1, 2)]
        var_eps = [sb(f"var_eps{n}", [128, TI]) for n in (1, 2)]
        rstd = [sb(f"rstd{n}", [128, TI]) for n in (1, 2)]
        xn = [sb(f"xn{n}", [128, TI, C]) for n in (1, 2)]
        hT = sb("hT", [C, T]); h2T = sb("h2T", [C, T])
        qk_parts = sb("qk_parts_sb", [128, 2, PARTS, T], BF16)
        qk_rest = sb("qk_rest", [128, 2, T])
        mx = sb("mx", [128, NH, TI])
        mx_all = sb("mx_all", [128, NH * TI])
        mx_parts = sb("mx_parts_sb", [128, PARTS, NH * TI], BF16)
        mx_rest = sb("mx_rest", [128, 2, NH * TI])
        mx_rows = sb("mx_rows", [PARTS * NH * TI, 128], BF16)
        probs = sb("probs", [128, 6, 512])
        v_ones = sb("v_ones", [128, TI, NH, 32])
        yT = sb("yT", [128, 2, T])
        y_rec = sb("y_rec", [128, TI, 4]); y = sb("y", [128, TI, NH, HS])
        y_gated = sb("y_gated", [128, TI, C])
        r_max = sb("r_max", [128, TI]); r_in = sb("r_in", [128, TI, E]); r_exp = sb("r_exp", [128, TI, E])
        r_sum = sb("r_sum", [128, TI]); r_rec = sb("r_rec", [128, TI]); score = sb("score", [128, TI, E])
        biased = sb("biased", [128, TI, E]); above = sb("above", [128, TI, E, E])
        equal = sb("equal", [128, TI, E, E]); rank = sb("rank", [128, TI, E]); gates = sb("gates", [128, TI, E])
        g_tanh = sb("g_tanh", [128, 2, T]); act_g = sb("act_g", [128, 2, T])
        hidden = sb("hidden", [128, 2, T])
        f_part = sb("f_part", [128, 2, TI, C]); f_sum = sb("f_sum", [128, TI, C])
        f_out = sb("f_out", [128, TI, C]); o_sb = sb("o_sb", [128, TI, C])

        bank = [ctx.enter_context(nc.psum_tensor(f"bank{i}", [128, 512], F32)) for i in range(8)]
        P_EXP, P_UP, P_DOWN, P_FRONT, P_BACK = bank[1:3], bank[3:5], bank[5], bank[6], bank[7]

        def max_bank(b, u):
            if isinstance(b, int) and b < N_SPREAD:
                return bank[(0, 3, 4)[u % 3]], 3
            return bank[0], 1

        names = """ld_small ld_c ld_mod ld_route ld_x ld_x0 ld_up ld_down ld_ones k_ident k_mask k_rest k_fill
            t_setup cT_saved e_setup w_ready k_rows m_tanh m_sig m_silu g_ready g_step g_rows_ready g_wide g_saved
            ln1_stats ln1_mv ln1_ve ln1_rstd ln1_norm xT_ready hT_ready qk_ready part1 rest1 part2 part3
            v_ready v_saved qk_stored stacked s1_ready s1_max m_all m_part1 m_rest1 m_part2 m_rest2 m_part3
            mT_ready mT_saved m_stacked
            v_placed s2_ready s2_exp s2_masked pv_ready yT_saved ytr_ready y_recip y_norm y_gate x2_ready
            ln2_stats ln2_mv ln2_ve ln2_rstd ln2_norm h2x_ready h2T_ready r_ready r_maxed r_shifted r_exped
            r_summed r_inv r_biased r_above r_equal r_tied r_counted r_ranked r_scored gates_ready
            up_ready tanhed silued hid_ready down_ready scaled added f_gated o_ready stored"""
        S = {n: sem(n) for n in names.split()}
        block = ctx.enter_context(nc.Block())
        N_SETUP = 4
        N_SPREAD = 3

        @block.sync
        def _(sp):
            for dst, src in ((wuq, W_uq), (wdq, W_dq), (wuk, W_uk), (wdkv, W_dkv)):
                sp.dma_start(dst[:], src).then_inc(S["ld_small"], DMA)
            sp.dma_start(w_up[:, 0:E, 0, :], w1.rearrange("e d h -> d e h")).then_inc(S["ld_up"], DMA)
            sp.dma_start(w_up[:, 0:E, 1, :], w3.rearrange("e d h -> d e h")).then_inc(S["ld_up"], DMA)
            sp.dma_start(w_up[:, E, 0, :], sw1).then_inc(S["ld_up"], DMA)
            sp.dma_start(w_up[:, E, 1, :], sw3).then_inc(S["ld_up"], DMA)
            sp.dma_start(w_down[:, 0:E, :], w2.rearrange("e h d -> h e d")).then_inc(S["ld_down"], DMA)
            sp.dma_start(w_down[:, E, :], sw2).then_inc(S["ld_down"], DMA)
            sp.wait_ge(S["k_fill"], 1)
            for b in range(RING):
                sp.dma_start(k_stack[ROWS:MROWS, b * SPAN:(b + 1) * SPAN], ones_rows[:, :])\
                  .then_inc(S["ld_ones"], DMA)

            def slot(t):
                for s in range(STEPS):
                    for b, _ in due(t, s, V):
                        sp.wait_ge(S["part3"], at(b, 1))
                        sp.dma_start(qk_dram[bass.ds(b, 1)].rearrange("b s i r t -> r (b s i) t"),
                                     qk_parts[:].rearrange("r s i t -> r (s i) t")).then_inc(S["qk_stored"], DMA)
                        sp.wait_ge(S["qk_stored"], b * DMA + DMA)
                        wait(sp, S["s2_ready"], (b - RING + 1) * UNITS)
                        wait(sp, S["stacked"], b * 4 * DMA)
                        for i in range(PARTS):
                            src = qk_dram[bass.ds(b, 1), 0, i].rearrange("b (d h) t -> (b d) (h t)", d=HS)
                            sp.dma_start(q_stack[24 * i:24 * i + 24, ring(b)],
                                         src.unsqueeze(0).to_broadcast([PARTS, HS, SPAN])).then_inc(S["stacked"], DMA)
                        src = qk_dram[bass.ds(b, 1), 1].rearrange("b i (d h) t -> (b i d) (h t)", d=HS)
                        sp.dma_start(k_stack[0:ROWS, ring(b)],
                                     src.unsqueeze(0).to_broadcast([PARTS, PARTS * HS, SPAN]))\
                          .then_inc(S["stacked"], DMA)
                    for b, _ in due(t, s, OUT):
                        sp.wait_ge(S["o_ready"], at(b, 1))
                        sp.dma_start(out[bass.ds(b, 1)].rearrange("b (i p) c -> p (b i) c", p=128), o_sb[:, :, :])\
                          .then_inc(S["stored"], DMA)
            over_slots(sp, slot)
            sp.wait_ge(S["stored"], B * DMA)

        @block.gpsimd
        def _(pool):
            g = nc.gpsimd
            g.memset(ident[:], 0.0).then_inc(S["k_ident"], 1)
            g.memset(ident_bf[:], 0.0).then_inc(S["k_ident"], 1)
            pool.wait_ge(S["k_ident"], 2)
            for m in (ident, ident_bf):
                g.affine_select(out=m[:], in_=m[:], compare_op=ALU.not_equal, fill=1.0, base=0,
                                pattern=[[-1, 128]], channel_multiplier=1).then_inc(S["k_ident"], 1)
            g.memset(neg_half[:], -0.5).then_inc(S["k_rest"], 1)
            g.memset(causal[:], 0.0).then_inc(S["k_mask"], 1)
            g.memset(entry_row[:], 1.0).then_inc(S["k_rows"], 1)
            g.memset(earlier[:], 1.0).then_inc(S["k_rest"], 1)
            g.memset(v_ones[:], 0.0).then_inc(S["k_rest"], 1)
            pool.wait_ge(S["k_mask"], 1)
            g.affine_select(out=causal[:], in_=causal[:], compare_op=ALU.is_ge, fill=MASKED, base=0,
                            pattern=[[0, 4], [-1, 128]], channel_multiplier=1).then_inc(S["k_mask"], 1)
            pool.wait_ge(S["k_rows"], 1)
            g.affine_select(out=entry_row[:], in_=entry_row[:], compare_op=ALU.is_equal, fill=0.0, base=0,
                            pattern=[[-1, B], [0, 128]], channel_multiplier=1).then_inc(S["k_rows"], 1)
            pool.wait_ge(S["k_rest"], 3)
            g.affine_select(out=earlier[:], in_=earlier[:], compare_op=ALU.is_gt, fill=0.0, base=0,
                            pattern=[[1, E], [-1, E]], channel_multiplier=0).then_inc(S["k_rest"], 1)
            g.memset(v_ones[:, :, :, HS], 1.0).then_inc(S["k_rest"], 1)
            pool.wait_ge(S["k_rest"], 5)

            def inv_std(n, b):
                pool.wait_ge(S[f"ln{n}_mv"], at(b, 1))
                alone(pool)
                g.tensor_scalar(var_eps[n - 1][:], mean_var[n - 1][:, :, 1], EPS, None, ALU.add)\
                 .then_inc(S[f"ln{n}_ve"], 1)
                pool.wait_ge(S[f"ln{n}_ve"], at(b, 1))
                wait(pool, S[f"ln{n}_norm"], b)
                g.tensor_tensor(rstd[n - 1][:], var_eps[n - 1][:], neg_half[:], ALU.pow)\
                 .then_inc(S[f"ln{n}_rstd"], 1)

            def mask(b, u):
                pool.wait_ge(S["s2_exp"], at(b, UNITS, u))
                alone(pool)
                buf = probs[:, u % 6, :]
                v = buf.rearrange("k (h q) -> k h q", h=4) if u % 3 == 2 else \
                    buf.rearrange("k (h q) -> k h q", h=2)[:, :, 0:128]
                g.affine_select(out=v, in_=v, compare_op=ALU.is_ge, fill=0.0, base=0,
                                pattern=[[0, 4 if u % 3 == 2 else 2], [1, 128]], channel_multiplier=-1)\
                 .then_inc(S["s2_masked"], 1)

            def slot(t):
                for s in range(STEPS):
                    for b, _ in due(t, s, V):
                        pool.wait_ge(S["part2"], at(b, 1))
                        g.tensor_tensor(qk_parts[:, :, 2, :], qk_rest[:], qk_parts[:, :, 1, :], ALU.subtract)\
                         .then_inc(S["part3"], 1)
                    for b, _ in due(t, s, PV - 2):
                        pool.wait_ge(S["v_saved"], at(b, 1))
                        wait(pool, S["pv_ready"], b * GROUPS)
                        alone(pool)
                        g.tensor_copy(v_ones[:, :, :, 0:HS],
                                      v_sb[:, cols(b, TI * C)].rearrange("p (i h d) -> p i h d", i=TI, h=NH))\
                         .then_inc(S["v_placed"], 1)
                    for b, u in due(t, s, EXP, UNITS):
                        mask(b, u)
                    for b, n in due(t, s, ADD + 1, E):
                        pool.wait_ge(S["scaled"], at(b, X, n + 1))
                        wait(pool, S["added"], at(b, E, n - 1))
                        g.tensor_tensor(f_sum[:], f_sum[:], f_part[:, (n + 1) % 2], ALU.add)\
                         .then_inc(S["added"], 1)
                    for b, _ in due(t, s, OUT):
                        pool.wait_ge(S["added"], at(b, E, E - 1))
                        wait(pool, S["o_ready"], b)
                        g.tensor_tensor(f_out[:], f_sum[:],
                                        res_gates[:, cols(b, 2 * C, C, C)].unsqueeze(1).to_broadcast([128, TI, C]),
                                        ALU.mult).then_inc(S["f_gated"], 1)
                        pool.wait_ge(S["f_gated"], at(b, 1))
                        wait(pool, S["stored"], b * DMA)
                        g.tensor_tensor(o_sb[:].rearrange("p i c -> p (i c)"), f_out[:].rearrange("p i c -> p (i c)"),
                                        x2_sb[:, cols(b, TI * C)], ALU.add).then_inc(S["o_ready"], 1)
                    for b, _ in due(t, s, LN1):
                        if not (isinstance(b, int) and b == 0):
                            inv_std(1, b)
                    for b, _ in due(t, s, M_SPLIT):
                        m = mx_all[:]
                        pool.wait_ge(S["m_all"], at(b, 1))
                        wait(pool, S["mT_ready"], b)
                        alone(pool)
                        g.tensor_scalar(mx_parts[:, 0], m, -1.0, None, ALU.mult).then_inc(S["m_part1"], 1)
                        pool.wait_ge(S["m_part1"], at(b, 1))
                        g.tensor_tensor(mx_rest[:, 0], m, mx_parts[:, 0], ALU.add).then_inc(S["m_rest1"], 1)
                        pool.wait_ge(S["m_rest1"], at(b, 1))
                        alone(pool)
                        g.tensor_scalar(mx_parts[:, 1], mx_rest[:, 0], -1.0, None, ALU.mult)\
                         .then_inc(S["m_part2"], 1)
                        pool.wait_ge(S["m_part2"], at(b, 1))
                        g.tensor_tensor(mx_rest[:, 1], mx_rest[:, 0], mx_parts[:, 1], ALU.add)\
                         .then_inc(S["m_rest2"], 1)
                        pool.wait_ge(S["m_rest2"], at(b, 1))
                        alone(pool)
                        g.tensor_scalar(mx_parts[:, 2], mx_rest[:, 1], -1.0, None, ALU.mult)\
                         .then_inc(S["m_part3"], 1)
                    for b, _ in due(t, s, LN2):
                        inv_std(2, b)
                    for b, _ in due(t, s, RES):
                        if isinstance(b, int) and b < 2:
                            pool.wait_ge(S["g_saved"], 1 if b == 0 else 4)
                        pool.wait_ge(S["y_norm"], at(b, GROUPS, GROUPS - 1))
                        alone(pool)
                        g.tensor_tensor(y_gated[:], y[:].rearrange("p i h d -> p i (h d)"),
                                        res_gates[:, cols(b, 2 * C, 0, C)].unsqueeze(1).to_broadcast([128, TI, C]),
                                        ALU.mult).then_inc(S["y_gate"], 1)
                        pool.wait_ge(S["y_gate"], at(b, 1))
                        alone(pool)
                        g.tensor_tensor(x2_sb[:, cols(b, TI * C)], x_sb[:, cols(b, TI * C)],
                                        y_gated[:].rearrange("p i c -> p (i c)"), ALU.add)\
                         .then_inc(S["x2_ready"], 1)

            inv_std(1, 0)
            g.memset(ones_rows[:], 1.0).then_inc(S["k_fill"], 1)
            over_slots(pool, slot)

        @block.scalar
        def _(act):
            a = nc.scalar
            act.dma_start(c_sb[:], c).then_inc(S["ld_c"], DMA)
            act.dma_start(wo[:], W_o).then_inc(S["ld_small"], DMA)
            act.dma_start(wuv[:], W_uv).then_inc(S["ld_small"], DMA)
            k = B * TI // 4

            def load_x(n):
                act.dma_start(x_sb[:, n * k * C:(n + 1) * k * C].rearrange("p (i c) -> p i c", c=C),
                              x.rearrange("b (i p) c -> p (b i) c", p=128)[:, n * k:(n + 1) * k, :])\
                   .then_inc(S["ld_x"] if n else S["ld_x0"], DMA)

            load_x(0)
            act.dma_start(wm[:], wmod).then_inc(S["ld_mod"], DMA)
            act.wait_ge(S["cT_saved"], 1)
            a.activation(c_tanh[:], cT[:], ACT.Tanh, scale=0.5).then_inc(S["m_tanh"], 1)
            for n in range(1, 4):
                load_x(n)
            act.dma_start(router[:], router_w).then_inc(S["ld_route"], DMA)
            act.dma_start(bias[:], expert_bias.unsqueeze(0).to_broadcast([128, E])).then_inc(S["ld_route"], DMA)

            def exps(b, u):
                act.wait_ge(S["s2_ready"], at(b, UNITS, u))
                wait(act, S["pv_ready"], at(b, GROUPS, (u - 6) // 3))
                a.activation(probs[:, u % 6, :], P_EXP[u % 2][:], ACT.Exp, scale=SCALE).then_inc(S["s2_exp"], 1)

            def scale_output(b, n):
                act.wait_ge(S["down_ready"], at(b, X, n))
                if n == 1:
                    act.wait_ge(S["gates_ready"], at(b, 1))
                wait(act, S["added"], b * (X - 1) + n - 2)
                out_n = P_DOWN[:, 0:T].rearrange("p (i c) -> p i c", i=TI)
                if n == 0:
                    wait(act, S["f_gated"], b)
                    last = a.activation(f_sum[:], out_n, ACT.Copy)
                else:
                    for i in range(TI):
                        last = a.activation(f_part[:, n % 2, i], out_n[:, i], ACT.Copy,
                                            scale=gates[:, i, n - 1:n])
                last.then_inc(S["scaled"], 1)

            def slot(t):
                for s in range(STEPS):
                    for b, n in due(t, s, ADD, X):
                        scale_output(b, n)
                    for b, _ in due(t, s, QK):
                        act.wait_ge(S["qk_ready"], at(b, 1))
                        wait(act, S["qk_stored"], b * DMA)
                        a.activation(qk_parts[:, :, 0, :], P_FRONT[:].rearrange("p (s t) -> p s t", s=2), ACT.Copy)\
                         .then_inc(S["part1"], 1)
                    for b, _ in due(t, s, V):
                        act.wait_ge(S["rest1"], at(b, 1))
                        a.activation(qk_parts[:, :, 1, :], qk_rest[:], ACT.Copy).then_inc(S["part2"], 1)
                    for b, u in due(t, s, EXP, UNITS):
                        exps(b, u)
                    for b, n in due(t, s, UP, X):
                        act.wait_ge(S["up_ready"], at(b, X, n))
                        wait(act, S["silued"], at(b, X, n - 2))
                        a.activation(g_tanh[:, n % 2, :], P_UP[n % 2][:, 0:T], ACT.Tanh, scale=0.5)\
                         .then_inc(S["tanhed"], 1)
                    for b, _ in due(t, s, H_T):
                        act.wait_ge(S["h2x_ready"], at(b, 1))
                        wait(act, S["up_ready"], b * X)
                        wait(act, S["r_ready"], b)
                        a.activation(h2T[:], P_FRONT[:, 0:T], ACT.Identity, bias=mod[:, 2, bass.ds(b, 1)],
                                     scale=mod[:, 3, bass.ds(b, 1)]).then_inc(S["h2T_ready"], 1)
                    for b, _ in due(t, s, ROUTE):
                        act.wait_ge(S["r_shifted"], at(b, 1))
                        wait(act, S["r_scored"], b)
                        a.activation(r_exp[:], r_in[:], ACT.Exp).then_inc(S["r_exped"], 1)
                    for b, g in due(t, s, PV, GROUPS, 3):
                        act.wait_ge(S["pv_ready"], at(b, GROUPS, g))
                        wait(act, S["ytr_ready"], at(b, GROUPS, g - 2))
                        a.activation(yT[:, g % 2, :], P_BACK[:, 0:T], ACT.Copy).then_inc(S["yT_saved"], 1)
                    for b, _ in due(t, s, X_T):
                        act.wait_ge(S["xT_ready"], at(b, 1))
                        wait(act, S["v_ready"], b)
                        a.activation(hT[:], P_FRONT[:, 0:T], ACT.Identity, bias=mod[:, 0, bass.ds(b, 1)],
                                     scale=mod[:, 1, bass.ds(b, 1)]).then_inc(S["hT_ready"], 1)
                    if isinstance(t, int) and t == 3 and s % 3 == 1:
                        n = s // 3
                        act.wait_ge(S["g_wide"], n + 1)
                        a.activation(res_gates[:, n * 4 * C:(n + 1) * 4 * C], bank[5][:], ACT.Copy)\
                         .then_inc(S["g_saved"], 1)
                    for b, _ in due(t, s, M_T):
                        act.wait_ge(S["mT_ready"], at(b, 1))
                        wait(act, S["m_stacked"], b * DMA)
                        a.activation(mx_rows[:], P_FRONT[0:96, 0:64].bitcast(BF16), ACT.Copy)\
                         .then_inc(S["mT_saved"], 1)
                        act.wait_ge(S["mT_saved"], at(b, 1))
                        act.dma_start(q_stack[ROWS:MROWS, ring(b)], mx_rows[:, :]).then_inc(S["m_stacked"], DMA)
            act.wait_ge(S["e_setup"], N_SETUP)
            over_slots(act, slot)

        @block.vector
        def _(dve):
            v = nc.vector
            def residual_gates():
                src = bank[5][0:B, 0:2 * C]
                dve.wait_ge(S["g_ready"], 1)
                v.tensor_scalar(g_sign[:], src, 0.0, 2.0, ALU.is_ge, ALU.mult)
                v.tensor_scalar(g_neg[:], src, -1.0, None, ALU.mult).then_inc(S["g_step"], 1)
                dve.wait_ge(S["g_step"], 1)
                v.scalar_tensor_tensor(g_abs[:], g_neg[:], 0.25, src, ALU.max, ALU.max).then_inc(S["g_step"], 1)
                dve.wait_ge(S["g_step"], 2)
                v.scalar_tensor_tensor(g_rows[:], g_sign[:], -1.0, g_abs[:], ALU.add, ALU.mult)\
                 .then_inc(S["g_step"], 1)
                dve.wait_ge(S["g_step"], 3)
                v.tensor_scalar(g_rows[:, C:2 * C], g_rows[:, C:2 * C], 0.5, None, ALU.mult)\
                 .then_inc(S["g_rows_ready"], 1)

            def ln_stats(n, b, src):
                wait(dve, S[f"ln{n}_norm"], b)
                alone(dve)
                for i in range(TI):
                    last = v.bn_stats(stats[n - 1][:, i], src[:, cols(b, TI * C, i * C, C)])
                last.then_inc(S[f"ln{n}_stats"], 1)
                dve.wait_ge(S[f"ln{n}_stats"], at(b, 1))
                alone(dve)
                for i in range(TI):
                    last = v.bn_aggr(mean_var[n - 1][:, i], stats[n - 1][:, i])
                last.then_inc(S[f"ln{n}_mv"], 1)

            def ln_norm(n, b, src, used):
                dve.wait_ge(S[f"ln{n}_rstd"], at(b, 1))
                wait(dve, S[used], b)
                for i in range(TI):
                    last = v.tensor_scalar(xn[n - 1][:, i], src[:, cols(b, TI * C, i * C, C)],
                                           mean_var[n - 1][:, i, 0:1], rstd[n - 1][:, i:i + 1],
                                           ALU.subtract, ALU.mult)
                last.then_inc(S[f"ln{n}_norm"], 1)

            dve.wait_ge(S["t_setup"], 1)
            v.tensor_copy(cT[:], bank[0][:, 0:B]).then_inc(S["cT_saved"], 1)
            v.tensor_copy(wuqT[:], bank[0][0:32, 128:256])
            v.tensor_copy(woT[:], bank[0][:, 256:384]).then_inc(S["e_setup"], 1)
            dve.wait_ge(S["ld_x0"], DMA)
            ln_stats(1, 0, x_sb)
            dve.wait_ge(S["t_setup"], 2)
            v.tensor_copy(w_q[:], bank[1][:, 128:256])
            v.tensor_copy(v_eff[:], bank[1][0:32, 256:384]).then_inc(S["e_setup"], 1)
            dve.wait_ge(S["m_tanh"], 1)
            v.tensor_scalar(c_sig[:], c_tanh[:], 1.0, 0.5, ALU.add, ALU.mult).then_inc(S["m_sig"], 1)
            dve.wait_ge(S["m_sig"], 1)
            v.tensor_tensor(c_silu[:], c_sig[:], cT[:], ALU.mult).then_inc(S["m_silu"], 1)
            v.tensor_copy(w_qT[:].rearrange("c (d h) -> c d h", d=HS),
                          bank[1][:, 0:128].rearrange("c (h d) -> c d h", h=NH)).then_inc(S["w_ready"], 1)
            dve.wait_ge(S["t_setup"], 3)
            v.tensor_copy(k_effT[:], bank[2][0:32, 0:128]).then_inc(S["e_setup"], 1)
            ln_norm(1, 0, x_sb, "xT_ready")
            dve.wait_ge(S["t_setup"], 4)
            for n, plus in enumerate((0.0, 1.0, 0.0, 1.0)):
                last = v.tensor_scalar(mod[:, n], bank[4][:, n * B:n * B + B], plus, None, ALU.add)
            last.then_inc(S["e_setup"], 1)
            dve.wait_ge(S["t_setup"], 5)
            v.tensor_copy(w_kT[:].rearrange("c (d h) -> c d h", d=HS),
                          bank[3][:, 0:128].rearrange("c (h d) -> c d h", h=NH))
            v.tensor_copy(w_vT[:], bank[3][:, 128:256]).then_inc(S["w_ready"], 1)

            def row_max(b, u):
                dve.wait_ge(S["s1_ready"], at(b, UNITS, u))
                if u == 0:
                    wait(dve, S["m_all"], b)
                if u < 4:
                    dst, n = mx[:, 4 * u:4 * u + 4, 0], 4
                else:
                    dst, n = mx[:, 2 * (u - 4):2 * (u - 4) + 2, 1], 2
                v.tensor_reduce(dst, max_bank(b, u)[0][:].rearrange("p (h k) -> p h k", h=n), AX.X, ALU.max)\
                 .then_inc(S["s1_max"], 1)
                if u == UNITS - 1:
                    dve.wait_ge(S["s1_max"], at(b, UNITS, u))
                    wait(dve, S["m_rest1"], b)
                    wait(dve, S["m_part1"], b)
                    v.tensor_copy(mx_all[:], mx[:].rearrange("p h i -> p (h i)")).then_inc(S["m_all"], 1)

            def hidden_of(b, n):
                dve.wait_ge(S["silued"], at(b, X, n))
                wait(dve, S["down_ready"], at(b, X, n - 2))
                v.tensor_tensor(hidden[:, n % 2, :], P_UP[n % 2][:, T:2 * T], act_g[:, n % 2, :], ALU.mult)\
                 .then_inc(S["hid_ready"], 1)

            def step(sem_name, b, instruction):
                instruction.then_inc(S[sem_name], 1)
                dve.wait_ge(S[sem_name], at(b, 1))

            def shift_logits(b):
                src = P_FRONT[:, 0:TI * E].rearrange("p (i e) -> p i e", i=TI)
                dve.wait_ge(S["r_ready"], at(b, 1))
                step("r_maxed", b, v.tensor_reduce(r_max[:], src, AX.X, ALU.max))
                v.tensor_tensor(r_in[:], src, r_max[:].unsqueeze(2).to_broadcast([128, TI, E]),
                                ALU.subtract).then_inc(S["r_shifted"], 1)

            def softmax(b):
                dve.wait_ge(S["r_exped"], at(b, 1))
                step("r_summed", b, v.tensor_reduce(r_sum[:], r_exp[:], AX.X, ALU.add))
                step("r_inv", b, v.reciprocal(r_rec[:], r_sum[:]))
                step("r_scored", b, v.tensor_tensor(score[:], r_exp[:],
                                                    r_rec[:].unsqueeze(2).to_broadcast([128, TI, E]), ALU.mult))
                step("r_biased", b, v.tensor_tensor(biased[:], score[:],
                                                    bias[:].unsqueeze(1).to_broadcast([128, TI, E]), ALU.add))

            def compare(b):
                other = biased[:].unsqueeze(2).to_broadcast([128, TI, E, E])
                own = biased[:].unsqueeze(3).to_broadcast([128, TI, E, E])
                v.tensor_tensor(above[:], other, own, ALU.is_gt).then_inc(S["r_above"], 1)
                step("r_equal", b, v.tensor_tensor(equal[:], other, own, ALU.is_equal))
                step("r_tied", b, v.tensor_tensor(equal[:], equal[:],
                                                  earlier[:].unsqueeze(1).to_broadcast([128, TI, E, E]), ALU.mult))
                step("r_counted", b, v.tensor_tensor(above[:], above[:], equal[:], ALU.add))

            def choose(b):
                step("r_ranked", b, v.tensor_reduce(rank[:], above[:], AX.X, ALU.add))
                wait(dve, S["scaled"], b * X)
                v.scalar_tensor_tensor(gates[:], rank[:], 1.5, score[:], ALU.is_lt, ALU.mult)\
                 .then_inc(S["gates_ready"], 1)

            def slot(t):
                for s in range(STEPS):
                    for b, n in due(t, s, HID, X):
                        hidden_of(b, n)
                    for b, _ in due(t, s, QK):
                        dve.wait_ge(S["part1"], at(b, 1))
                        wait(dve, S["part3"], b)
                        v.tensor_tensor(qk_rest[:], P_FRONT[:].rearrange("p (s t) -> p s t", s=2),
                                        qk_parts[:, :, 0, :], ALU.subtract).then_inc(S["rest1"], 1)
                    for b, _ in due(t, s, SOFTMAX):
                        softmax(b)
                    for b, u in due(t, s, MAX, UNITS):
                        row_max(b, u)
                    for b, _ in due(t, s, LN2_NORM):
                        ln_norm(2, b, x2_sb, "h2x_ready")
                    for b, _ in due(t, s, LN1_NORM):
                        if not (isinstance(b, int) and b == 0):
                            ln_norm(1, b, x_sb, "xT_ready")
                    for b, n in due(t, s, UP, X):
                        dve.wait_ge(S["tanhed"], at(b, X, n))
                        wait(dve, S["hid_ready"], at(b, X, n - 2))
                        v.scalar_tensor_tensor(act_g[:, n % 2, :], g_tanh[:, n % 2, :], 1.0,
                                               P_UP[n % 2][:, 0:T], ALU.add, ALU.mult)\
                         .then_inc(S["silued"], 1)
                    for b, _ in due(t, s, V):
                        dve.wait_ge(S["v_ready"], at(b, 1))
                        v.tensor_copy(v_sb[:, cols(b, TI * C)], P_FRONT[:, 0:TI * C]).then_inc(S["v_saved"], 1)
                    for b, g in due(t, s, Y_T, GROUPS, 3):
                        src = P_BACK[:, 0:T].rearrange("p (i h r) -> p i h r", i=TI, h=4)
                        dve.wait_ge(S["ytr_ready"], at(b, GROUPS, g))
                        wait(dve, S["y_norm"], at(b, GROUPS, g - 1))
                        v.reciprocal(y_rec[:], src[:, :, :, HS]).then_inc(S["y_recip"], 1)
                        dve.wait_ge(S["y_recip"], at(b, GROUPS, g))
                        if g == 0:
                            wait(dve, S["y_gate"], b)
                        v.tensor_tensor(y[:, :, 4 * g:4 * g + 4, :], src[:, :, :, 0:HS],
                                        y_rec[:].unsqueeze(3).to_broadcast([128, TI, 4, HS]), ALU.mult)\
                         .then_inc(S["y_norm"], 1)
                    for b, _ in due(t, s, LN2):
                        dve.wait_ge(S["x2_ready"], at(b, 1))
                        ln_stats(2, b, x2_sb)
                    for b, _ in due(t, s, ROUTE):
                        shift_logits(b)
                    for b, _ in due(t, s, COMPARE):
                        compare(b)
                    for b, _ in due(t, s, GATES):
                        choose(b)
                    for b, _ in due(t, s, LN1):
                        if not (isinstance(b, int) and b == 0):
                            dve.wait_ge(S["ld_x"], 3 * DMA)
                            ln_stats(1, b, x_sb)
                    if isinstance(t, int) and t == 0 and s == X_T + EARLY:
                        residual_gates()
            over_slots(dve, slot)

        @block.tensor
        def _(pe):
            mm, tr = nc.tensor.matmul, nc.tensor.transpose
            pe.wait_ge(S["k_ident"], 4)
            pe.wait_ge(S["ld_small"], 6 * DMA)
            pe.wait_ge(S["ld_c"], DMA)
            tr(bank[0][:, 0:B], c_sb[:], ident[0:B, 0:B])
            tr(bank[0][0:32, 128:256], wuq[:], ident[:])
            tr(bank[0][:, 256:384], wo[:], ident[:]).then_inc(S["t_setup"], 1)
            pe.wait_ge(S["e_setup"], 1)
            mm(bank[1][:, 128:256], wuqT[:], wdq[:], start=True, stop=True)
            mm(bank[1][0:32, 256:384], wuv[:], woT[:], start=True, stop=True)
            mm(bank[1][:, 0:128], wdq[:], wuqT[:], start=True, stop=True).then_inc(S["t_setup"], 1)
            pe.wait_ge(S["e_setup"], 2)
            mm(bank[2][0:32, 0:128], wuk[:], w_q[:], start=True, stop=True).then_inc(S["t_setup"], 1)
            pe.wait_ge(S["m_silu"], 1)
            pe.wait_ge(S["ld_mod"], DMA)
            for n, s in enumerate((0, 1, 3, 4)):
                last = mm(bank[4][:, n * B:n * B + B], wm[:, s * C:(s + 1) * C], c_silu[:], start=True, stop=True)
            last.then_inc(S["t_setup"], 1)
            pe.wait_ge(S["e_setup"], 3)
            mm(bank[3][:, 0:128], wdkv[:], k_effT[:], start=True, stop=True)
            mm(bank[3][:, 128:256], wdkv[:], v_eff[:], start=True, stop=True).then_inc(S["t_setup"], 1)

            def widen_gates(n):
                pe.wait_ge(S["g_rows_ready"], 1)
                pe.wait_ge(S["k_rows"], 2)
                wait(pe, S["g_saved"], n)
                for j in range(2):
                    last = mm(bank[5][:, j * 2 * C:(j + 1) * 2 * C], entry_row[:, 2 * n + j, :],
                              g_rows[:], start=True, stop=True)
                last.then_inc(S["g_wide"], 1)

            front = {"x": (X_T, S["hT_ready"], 1, 0), "qk": (QK, S["rest1"], 1, 0), "v": (V, S["v_saved"], 1, 0),
                     "h": (H_T, S["h2T_ready"], 1, 0), "logits": (ROUTE, S["r_shifted"], 1, 0),
                     "m": (M_T, S["mT_saved"], 1, 0)}
            back = {**{f"pv{g}": (PV + 3 * g, S["yT_saved"], GROUPS, g) for g in range(GROUPS)},
                    **{f"y{g}": (Y_T + 3 * g, S["y_norm"], GROUPS, g) for g in range(GROUPS)}}

            def max_unit(b, u):
                place, banks = max_bank(b, u)
                wait(pe, S["s1_max"], b * UNITS + u + 1 - banks)
                if u == 0:
                    pe.wait_ge(S["stacked"], b * 4 * DMA + 4 * DMA)
                if u < 4:
                    mm(place[:], ident_bf[:], causal[:].rearrange("p h k -> p (h k)"), start=True, stop=False,
                       skip_group_check=True)
                    for j in range(4):
                        h = 4 * u + j
                        last = mm(place[:, j * 128:j * 128 + 128], q_stack[0:ROWS, ring(b, h * T, 128)],
                                  k_stack[0:ROWS, ring(b, h * T, 128)], start=False, stop=(j == 3),
                                  skip_group_check=True)
                else:
                    mm(place[:].rearrange("p (h k) -> p h k", h=2)[:, :, 128:256], ident_bf[:], causal[:, 0:2, :],
                       start=True, stop=False, skip_group_check=True)
                    for j in range(2):
                        h = 2 * (u - 4) + j
                        last = mm(place[:, j * T:j * T + T], q_stack[0:ROWS, ring(b, h * T + 128, 128)],
                                  k_stack[0:ROWS, ring(b, h * T, T)], start=False, stop=(j == 1),
                                  skip_group_check=True)
                last.then_inc(S["s1_ready"], 1)

            def exp_unit(b, u):
                wait(pe, S["s2_exp"], b * UNITS + u - 1)
                if u == 0:
                    pe.wait_ge(S["m_stacked"], b * DMA + DMA)
                    if isinstance(b, int) and b == 0:
                        pe.wait_ge(S["ld_ones"], RING * DMA)
                g, r = divmod(u, 3)
                if r < 2:
                    for j in range(2):
                        h = 4 * g + 2 * r + j
                        last = mm(P_EXP[u % 2][:, j * T:j * T + T], k_stack[:, ring(b, h * T, 128)],
                                  q_stack[:, ring(b, h * T, T)], start=True, stop=True)
                else:
                    for j in range(4):
                        h = 4 * g + j
                        last = mm(P_EXP[u % 2][:, j * 128:j * 128 + 128],
                                  k_stack[:, ring(b, h * T + 128, 128)],
                                  q_stack[:, ring(b, h * T + 128, 128)], start=True, stop=True)
                last.then_inc(S["s2_ready"], 1)

            def probs_v(b, g):
                pe.wait_ge(S["s2_masked"], at(b, UNITS, 3 * g + 2))
                if g == 0:
                    pe.wait_ge(S["v_placed"], at(b, 1))
                wait_turn(pe, back, f"pv{g}", b)
                for j in range(4):
                    unit = probs[:, (3 * g + 2) % 6, :]
                    mm(P_BACK[32 * j:32 * j + 32, 128:T], v_ones[:, 1, 4 * g + j, :],
                       unit[:, j * 128:j * 128 + 128], start=True, stop=False, skip_group_check=True)
                for j in range(4):
                    unit = probs[:, (3 * g + j // 2) % 6, :]
                    last = mm(P_BACK[32 * j:32 * j + 32, 0:T], v_ones[:, 0, 4 * g + j, :],
                              unit[:, (j % 2) * T:(j % 2) * T + T], start=False, stop=True,
                              skip_group_check=True)
                last.then_inc(S["pv_ready"], 1)

            def y_back(b, g):
                pe.wait_ge(S["yT_saved"], at(b, GROUPS, g))
                wait_turn(pe, back, f"y{g}", b)
                for i in range(TI):
                    last = tr(P_BACK[:, i * 128:i * 128 + 128], yT[:, g % 2, i * 128:i * 128 + 128], ident[:])
                last.then_inc(S["ytr_ready"], 1)

            def slot(t):
                for s in range(STEPS):
                    for b, u in due(t, s, EXP, UNITS):
                        exp_unit(b, u)
                    for b, _ in due(t, s, H_T):
                        pe.wait_ge(S["ln2_norm"], at(b, 1))
                        wait_turn(pe, front, "h", b)
                        for i in range(TI):
                            last = tr(P_FRONT[:, i * 128:i * 128 + 128], xn[1][:, i, :], ident[:])
                        last.then_inc(S["h2x_ready"], 1)
                    for b, n in due(t, s, UP, X):
                        e = (n - 1) % X
                        if isinstance(b, int) and b == 0:
                            pe.wait_ge(S["ld_up"], 4 * DMA)
                            if n < 2:
                                pe.wait_ge(S["s1_max"], N_SPREAD * UNITS - 1 + n)
                        pe.wait_ge(S["h2T_ready"], at(b, 1))
                        wait(pe, S["hid_ready"], at(b, X, n - 2))
                        for w in range(2):
                            last = mm(P_UP[n % 2][:, w * T:(w + 1) * T], w_up[:, e, w, :], h2T[:],
                                      start=True, stop=True)
                        last.then_inc(S["up_ready"], 1)
                    for b, u in due(t, s, MAX, UNITS):
                        max_unit(b, u)
                    for b, _ in due(t, s, X_T):
                        pe.wait_ge(S["ln1_norm"], at(b, 1))
                        wait_turn(pe, front, "x", b)
                        for i in range(TI):
                            last = tr(P_FRONT[:, i * 128:i * 128 + 128], xn[0][:, i, :], ident[:])
                        last.then_inc(S["xT_ready"], 1)
                    for b, _ in due(t, s, QK):
                        pe.wait_ge(S["hT_ready"], at(b, 1))
                        if isinstance(b, int) and b == 0:
                            pe.wait_ge(S["w_ready"], 2)
                        mm(P_FRONT[:, 0:T], w_qT[:], hT[:], start=True, stop=True)
                        mm(P_FRONT[:, T:2 * T], w_kT[:], hT[:], start=True, stop=True).then_inc(S["qk_ready"], 1)
                    for b, _ in due(t, s, V):
                        wait_turn(pe, front, "v", b)
                        for i in range(TI):
                            last = mm(P_FRONT[:, i * C:i * C + C], hT[:, i * 128:i * 128 + 128], w_vT[:],
                                      start=True, stop=True)
                        last.then_inc(S["v_ready"], 1)
                    for b, n in due(t, s, DOWN, X):
                        e = (n - 1) % X
                        pe.wait_ge(S["hid_ready"], at(b, X, n))
                        wait(pe, S["scaled"], at(b, X, n - 1))
                        if isinstance(b, int) and b == 0 and n == 0:
                            pe.wait_ge(S["ld_down"], 2 * DMA)
                            pe.wait_ge(S["g_saved"], 4)
                        for i in range(TI):
                            last = mm(P_DOWN[:, i * C:i * C + C],
                                      hidden[:, n % 2, i * 128:i * 128 + 128], w_down[:, e, :],
                                      start=True, stop=True)
                        last.then_inc(S["down_ready"], 1)
                    for b, g in due(t, s, PV, GROUPS, 3):
                        probs_v(b, g)
                    for b, g in due(t, s, Y_T, GROUPS, 3):
                        y_back(b, g)
                    for b, _ in due(t, s, ROUTE):
                        pe.wait_ge(S["h2T_ready"], at(b, 1))
                        wait_turn(pe, front, "logits", b)
                        if isinstance(b, int) and b == 0:
                            pe.wait_ge(S["ld_route"], 2 * DMA)
                        for i in range(TI):
                            last = mm(P_FRONT[:, i * E:i * E + E], h2T[:, i * 128:i * 128 + 128], router[:],
                                      start=True, stop=True)
                        last.then_inc(S["r_ready"], 1)
                    for b, _ in due(t, s, M_T):
                        pe.wait_ge(S["m_part3"], at(b, 1))
                        wait_turn(pe, front, "m", b)
                        tr(P_FRONT[0:96, 0:64].bitcast(BF16), mx_parts[:].rearrange("p i m -> p (i m)"),
                           ident_bf[:]).then_inc(S["mT_ready"], 1)
                    if isinstance(t, int) and t == 0 and s == V:
                        for j, part in enumerate((2, 5)):
                            last = mm(bank[5][0:B, j * C:(j + 1) * C], c_silu[:], wm[:, part * C:(part + 1) * C],
                                      start=True, stop=True)
                        last.then_inc(S["g_ready"], 1)
                    if isinstance(t, int) and t == 3 and s % 3 == 1:
                        widen_gates(s // 3)
            pe.wait_ge(S["k_mask"], 2)
            over_slots(pe, slot)


_INS = ['L0_attn_x', 'L0_attn_W_dq', 'L0_attn_W_uq', 'L0_attn_W_dkv', 'L0_attn_W_uk', 'L0_attn_W_uv', 'L0_attn_W_o',
        'L0_ffn_router_w', 'L0_ffn_expert_bias', 'L0_ffn_w1', 'L0_ffn_w2', 'L0_ffn_w3', 'L0_ffn_sw1', 'L0_ffn_sw2',
        'L0_ffn_sw3', 'L0_c', 'L0_wmod']


def kernel(**inputs):
    import numpy as np
    import concourse.bacc as bacc
    from concourse.bass_utils import run_bass_kernel_spmd

    nc = bacc.Bacc("TRN2", target_bir_lowering=False, num_devices=1)
    arrays, args = {}, []
    for name in _INS:
        a = np.ascontiguousarray(inputs[name])
        arrays[f"in_{name}"] = a
        args.append(nc.dram_tensor(f"in_{name}", a.shape, mybir.dt.from_np(a.dtype), kind="ExternalInput").ap())
    out = nc.dram_tensor("out", (B, T, C), F32, kind="ExternalOutput").ap()
    build(nc, *args, out)
    return run_bass_kernel_spmd(nc, [arrays], core_ids=[0]).results[0]["out"]
```
